# Optimizing a Trainium2 kernel written in Bass

```python
import numpy as np
import jax
import jax.numpy as jnp

def _softmax(x, axis=-1):
    return jax.nn.softmax(x, axis=axis)

def _gelu(x):
    return jax.nn.gelu(x, approximate=True)

def _silu(x):
    return jax.nn.silu(x)

def _sigmoid(x):
    return jax.nn.sigmoid(x)

def _layernorm(x, axis=-1, eps=1e-05):
    m = jnp.mean(x, axis=axis, keepdims=True)
    v = jnp.var(x, axis=axis, keepdims=True)
    return (x - m) / jnp.sqrt(v + eps)

def _scatter_add(tgt, idx, src, axis=0):
    return tgt.at[idx].add(src)

def _segment_sum(src, seg, n):
    return jax.ops.segment_sum(src, seg, n)
kernel_name = 'mk_gnn_preln_d4_gnn_r32_f08f24'

def setup_inputs(seed: int=0):
    np.random.seed(seed)
    _w = jnp.asarray

    def _rec_inputs():
        import jax
        import jax.numpy as jnp
        _gk = jax.random.key(seed)
        x = -0.0003713 + 1 * jax.random.normal(jax.random.fold_in(_gk, 1), (3125, 256), jnp.float32)
        _s = jax.random.randint(jax.random.fold_in(_gk, 2), (25000,), 0, 3125, jnp.int32)
        _d = jax.random.randint(jax.random.fold_in(_gk, 3), (25000,), 0, 3125, jnp.int32)
        _loop = jnp.arange(3125, dtype=jnp.int32)
        src = jnp.concatenate([_s, _d, _loop])
        dst = jnp.concatenate([_d, _s, _loop])
        _o = jnp.argsort(dst, stable=True)
        src = src[_o]
        dst = dst[_o]
        edge_type_4 = jax.random.randint(jax.random.fold_in(_gk, 13), (53125,), 0, 4, jnp.int32)
        edge_weight = jax.random.uniform(jax.random.fold_in(_gk, 14), (53125,), jnp.float32, 0.0, 0.999998)
        return (x, src, dst, edge_type_4, edge_weight)
    x, src, dst, edge_type_4, edge_weight = _rec_inputs()

    def _L0_gnn_setup():
        import jax, jax.numpy as jnp
        import numpy as np
        N = 50000
        E = 25000
        HIDDEN = 256
        HEADS = 8
        HEAD_DIM = HIDDEN // HEADS

        def _linear_params(key, fan_in, fan_out):
            k1, k2 = jax.random.split(key)
            s = 1.0 / np.sqrt(fan_in)
            W = jax.random.uniform(k1, (fan_in, fan_out), jnp.float32, -s, s)
            b = jax.random.uniform(k2, (fan_out,), jnp.float32, -s, s)
            return (W, b)
        key = jax.random.key(seed)
        ks = jax.random.split(key, 7)
        h = jax.random.normal(ks[0], (N, HIDDEN), jnp.float32)
        row = jnp.sort(jax.random.randint(ks[1], (E,), 0, N))
        col = jax.random.randint(ks[2], (E,), 0, N)
        Wq, bq = _linear_params(ks[3], HIDDEN, HIDDEN)
        Wk, bk = _linear_params(ks[4], HIDDEN, HIDDEN)
        Wv, bv = _linear_params(ks[5], HIDDEN, HIDDEN)
        Wo, bo = _linear_params(ks[6], HIDDEN, HIDDEN)
        return dict(h=h, row=row, col=col, Wq=Wq, bq=bq, Wk=Wk, bk=bk, Wv=Wv, bv=bv, Wo=Wo, bo=bo)
    _L0_gnn_all = _L0_gnn_setup()
    _L0_gnn_in = {k: v for k, v in _L0_gnn_all.items() if k in ('Wq', 'bq', 'Wk', 'bk', 'Wv', 'bv', 'Wo', 'bo')}
    del _L0_gnn_all

    def _L1_gnn_setup():
        import jax, jax.numpy as jnp
        import numpy as np
        N_NODES = 3125
        N_EDGES = 100000
        D_IN = 256
        D_OUT = 256
        LEAKY_SLOPE = 0.01
        key = jax.random.key(seed)
        ks = jax.random.split(key, 8)
        s_in = 1.0 / np.sqrt(D_IN)
        s_out = 1.0 / np.sqrt(D_OUT)
        return {'features': jax.random.normal(ks[0], (N_NODES, D_IN), dtype=jnp.float32), 'indices': jax.random.randint(ks[1], (2, N_EDGES), 0, N_NODES, dtype=jnp.int64), 'W_layer': jax.random.uniform(ks[2], (D_OUT, D_IN), jnp.float32, -s_in, s_in), 'b_layer': jax.random.uniform(ks[3], (D_OUT,), jnp.float32, -s_in, s_in), 'w_a1': jax.random.uniform(ks[4], (1, D_OUT), jnp.float32, -s_out, s_out), 'b_a1': jax.random.uniform(ks[5], (1,), jnp.float32, -s_out, s_out), 'w_a2': jax.random.uniform(ks[6], (1, D_OUT), jnp.float32, -s_out, s_out), 'b_a2': jax.random.uniform(ks[7], (1,), jnp.float32, -s_out, s_out)}
    _L1_gnn_all = _L1_gnn_setup()
    _L1_gnn_in = {k: v for k, v in _L1_gnn_all.items() if k in ('W_layer', 'b_layer', 'w_a1', 'b_a1', 'w_a2', 'b_a2')}
    del _L1_gnn_all

    def _L2_gnn_setup():
        import jax, jax.numpy as jnp
        import numpy as np
        N_NODES = 50000
        N_EDGES = 12500
        D_IN = 256
        D_OUT = 256
        N_REL = 4
        key = jax.random.key(seed)
        ks = jax.random.split(key, 7)
        x = jax.random.normal(ks[0], (N_NODES, D_IN), dtype=jnp.float32)
        src = jax.random.randint(ks[1], (N_EDGES,), 0, N_NODES, dtype=jnp.int32)
        dst = jax.random.randint(ks[2], (N_EDGES,), 0, N_NODES, dtype=jnp.int32)
        edge_type = jax.random.randint(ks[3], (N_EDGES,), 0, N_REL, dtype=jnp.int32)
        scale_in = 1.0 / np.sqrt(D_IN)
        self_W = jax.random.uniform(ks[4], (D_IN, D_OUT), dtype=jnp.float32, minval=-scale_in, maxval=scale_in)
        self_b = jax.random.uniform(ks[5], (D_OUT,), dtype=jnp.float32, minval=-scale_in, maxval=scale_in)
        rel_W = jax.random.uniform(ks[6], (N_REL, D_IN, D_OUT), dtype=jnp.float32, minval=-scale_in, maxval=scale_in)
        return {'x': x, 'src': src, 'dst': dst, 'edge_type': edge_type, 'self_W': self_W, 'self_b': self_b, 'rel_W': rel_W}
    _L2_gnn_all = _L2_gnn_setup()
    _L2_gnn_in = {k: v for k, v in _L2_gnn_all.items() if k in ('self_W', 'self_b', 'rel_W')}
    del _L2_gnn_all

    def _L3_gnn_setup():
        import jax, jax.numpy as jnp
        import numpy as np
        N_NODES = 50000
        N_EDGES = 25000
        IN_CH = 256
        OUT_CH = 256
        BN_EPS = 1e-05
        key = jax.random.key(seed)
        ks = jax.random.split(key, 5)
        x = jax.random.normal(ks[0], (N_NODES, IN_CH), dtype=jnp.float32)
        edge_index = jax.random.randint(ks[1], (2, N_EDGES), 0, N_NODES, dtype=jnp.int64)
        edge_attr = jax.random.uniform(ks[2], (N_EDGES,), dtype=jnp.float32)
        weight = jax.random.normal(ks[3], (IN_CH, OUT_CH), dtype=jnp.float32) / np.sqrt(IN_CH)
        bias = jnp.zeros((OUT_CH,), dtype=jnp.float32)
        bn_gamma = jnp.ones((OUT_CH,), dtype=jnp.float32)
        bn_beta = jnp.zeros((OUT_CH,), dtype=jnp.float32)
        return {'x': x, 'edge_attr': edge_attr, 'weight': weight, 'bias': bias, 'bn_gamma': bn_gamma, 'bn_beta': bn_beta, 'edge_index': edge_index}
    _L3_gnn_all = _L3_gnn_setup()
    _L3_gnn_in = {k: v for k, v in _L3_gnn_all.items() if k in ('weight', 'bias', 'bn_gamma', 'bn_beta')}
    del _L3_gnn_all
    return {'x': x, 'src': src, 'dst': dst, 'edge_type_4': edge_type_4, 'edge_weight': edge_weight, 'L0_gnn_Wq': _L0_gnn_in['Wq'], 'L0_gnn_bq': _L0_gnn_in['bq'], 'L0_gnn_Wk': _L0_gnn_in['Wk'], 'L0_gnn_bk': _L0_gnn_in['bk'], 'L0_gnn_Wv': _L0_gnn_in['Wv'], 'L0_gnn_bv': _L0_gnn_in['bv'], 'L0_gnn_Wo': _L0_gnn_in['Wo'], 'L0_gnn_bo': _L0_gnn_in['bo'], 'L1_gnn_W_layer': _L1_gnn_in['W_layer'], 'L1_gnn_b_layer': _L1_gnn_in['b_layer'], 'L1_gnn_w_a1': _L1_gnn_in['w_a1'], 'L1_gnn_b_a1': _L1_gnn_in['b_a1'], 'L1_gnn_w_a2': _L1_gnn_in['w_a2'], 'L1_gnn_b_a2': _L1_gnn_in['b_a2'], 'L2_gnn_self_W': _L2_gnn_in['self_W'], 'L2_gnn_self_b': _L2_gnn_in['self_b'], 'L2_gnn_rel_W': _L2_gnn_in['rel_W'], 'L3_gnn_weight': _L3_gnn_in['weight'], 'L3_gnn_bias': _L3_gnn_in['bias'], 'L3_gnn_bn_gamma': _L3_gnn_in['bn_gamma'], 'L3_gnn_bn_beta': _L3_gnn_in['bn_beta']}

def reference(x, src, dst, edge_type_4, edge_weight, L0_gnn_Wq, L0_gnn_bq, L0_gnn_Wk, L0_gnn_bk, L0_gnn_Wv, L0_gnn_bv, L0_gnn_Wo, L0_gnn_bo, L1_gnn_W_layer, L1_gnn_b_layer, L1_gnn_w_a1, L1_gnn_b_a1, L1_gnn_w_a2, L1_gnn_b_a2, L2_gnn_self_W, L2_gnn_self_b, L2_gnn_rel_W, L3_gnn_weight, L3_gnn_bias, L3_gnn_bn_gamma, L3_gnn_bn_beta):
    import jax
    import jax.numpy as jnp

    def _L0_gnn_ref(h, row, col, Wq, bq, Wk, bk, Wv, bv, Wo, bo):
        import jax, jax.numpy as jnp
        import numpy as np
        N = 50000
        E = 25000
        HIDDEN = 256
        HEADS = 8
        HEAD_DIM = HIDDEN // HEADS

        def _linear_params(key, fan_in, fan_out):
            k1, k2 = jax.random.split(key)
            s = 1.0 / np.sqrt(fan_in)
            W = jax.random.uniform(k1, (fan_in, fan_out), jnp.float32, -s, s)
            b = jax.random.uniform(k2, (fan_out,), jnp.float32, -s, s)
            return (W, b)
        n = h.shape[0]
        scaling = HEAD_DIM ** (-0.5)
        q = (h @ Wq + bq).reshape(n, HEADS, HEAD_DIM) * scaling
        k = (h @ Wk + bk).reshape(n, HEADS, HEAD_DIM)
        v = (h @ Wv + bv).reshape(n, HEADS, HEAD_DIM)
        s = jnp.einsum('ehd,ehd->eh', q[row], k[col])
        m = jax.ops.segment_max(s, row, num_segments=n)
        p = jnp.exp(s - m[row])
        denom = jax.ops.segment_sum(p, row, num_segments=n)
        attn = p / denom[row]
        out = jax.ops.segment_sum(attn[:, :, None] * v[col], row, num_segments=n)
        return out.reshape(n, HIDDEN) @ Wo + bo

    def _L1_gnn_ref(features, indices, W_layer, b_layer, w_a1, b_a1, w_a2, b_a2):
        import jax, jax.numpy as jnp
        import numpy as np
        N_NODES = 3125
        N_EDGES = 100000
        D_IN = 256
        D_OUT = 256
        LEAKY_SLOPE = 0.01
        n = features.shape[0]
        h = features @ W_layer.T + b_layer
        a1 = (h @ w_a1.T + b_a1)[:, 0]
        a2 = (h @ w_a2.T + b_a2)[:, 0]
        row = indices[0]
        col = indices[1]
        v = jax.nn.leaky_relu(a1[row] + a2[col], negative_slope=LEAKY_SLOPE)
        m = jax.ops.segment_max(v, row, num_segments=n)
        ev = jnp.exp(v - m[row])
        s = jax.ops.segment_sum(ev, row, num_segments=n)
        att = ev / s[row]
        out = jax.ops.segment_sum(att[:, None] * h[col], row, num_segments=n)
        return out

    def _L2_gnn_ref(x, src, dst, edge_type, self_W, self_b, rel_W):
        import jax, jax.numpy as jnp
        import numpy as np
        N_NODES = 50000
        N_EDGES = 12500
        D_IN = 256
        D_OUT = 256
        N_REL = 4
        num_nodes = x.shape[0]
        x_src = x[src]
        msgs = jnp.zeros((src.shape[0], D_OUT), dtype=x.dtype)
        for r in range(N_REL):
            mask = (edge_type == r)[:, None]
            msgs = jnp.where(mask, x_src @ rel_W[r], msgs)
        agg = jax.ops.segment_sum(msgs, dst, num_segments=num_nodes)
        deg = jax.ops.segment_sum(jnp.ones_like(dst, dtype=x.dtype), dst, num_segments=num_nodes)
        deg = jnp.clip(deg, 1.0, None)[:, None]
        return jax.nn.relu(x @ self_W + self_b + agg / deg)

    def _L3_gnn_ref(x, edge_attr, weight, bias, bn_gamma, bn_beta, edge_index):
        import jax, jax.numpy as jnp
        import numpy as np
        N_NODES = 50000
        N_EDGES = 25000
        IN_CH = 256
        OUT_CH = 256
        BN_EPS = 1e-05
        n = x.shape[0]
        loop = jnp.arange(n, dtype=edge_index.dtype)
        src = jnp.concatenate([edge_index[0], loop])
        dst = jnp.concatenate([edge_index[1], loop])
        w = jnp.concatenate([edge_attr, jnp.ones((n,), x.dtype)])
        deg = jax.ops.segment_sum(w, dst, num_segments=n)
        dinv = jnp.where(deg > 0, jax.lax.rsqrt(deg), 0.0)
        norm = dinv[src] * w * dinv[dst]
        xw = x @ weight
        msgs = norm[:, None] * xw[src]
        agg = jax.ops.segment_sum(msgs, dst, num_segments=n) + bias
        mean = jnp.mean(agg, axis=0)
        var = jnp.mean(jnp.square(agg - mean), axis=0)
        y = (agg - mean) * jax.lax.rsqrt(var + BN_EPS) * bn_gamma + bn_beta
        return jax.nn.relu(y)
    edge_index = jnp.stack([src, dst])
    h = jnp.maximum(_layernorm(x, axis=-1), 0.0)
    x = x + _L0_gnn_ref(h, src, dst, L0_gnn_Wq, L0_gnn_bq, L0_gnn_Wk, L0_gnn_bk, L0_gnn_Wv, L0_gnn_bv, L0_gnn_Wo, L0_gnn_bo)
    h = jnp.maximum(_layernorm(x, axis=-1), 0.0)
    x = x + _L1_gnn_ref(h, edge_index, L1_gnn_W_layer, L1_gnn_b_layer, L1_gnn_w_a1, L1_gnn_b_a1, L1_gnn_w_a2, L1_gnn_b_a2)
    h = jnp.maximum(_layernorm(x, axis=-1), 0.0)
    x = x + _L2_gnn_ref(h, src, dst, edge_type_4, L2_gnn_self_W, L2_gnn_self_b, L2_gnn_rel_W)
    h = jnp.maximum(_layernorm(x, axis=-1), 0.0)
    x = x + _L3_gnn_ref(h, edge_weight, L3_gnn_weight, L3_gnn_bias, L3_gnn_bn_gamma, L3_gnn_bn_beta, edge_index)
    return x

_drawn_inputs = setup_inputs


def setup_inputs(seed=0):
    import zlib

    import numpy as np

    out = dict(_drawn_inputs(seed))
    spreads = {'L3_gnn_bias': (0.0, 0.8), 'L3_gnn_bn_gamma': (1.0, 0.2), 'L3_gnn_bn_beta': (0.0, 0.1)}
    factors = {'L0_gnn_Wq': 7.879,
     'L0_gnn_bq': 8.0,
     'L0_gnn_Wk': 8.0,
     'L0_gnn_bk': 8.0,
     'L0_gnn_bv': 3.149,
     'L1_gnn_w_a1': 7.643,
     'L1_gnn_w_a2': 8.0}
    for name, (base, spread) in spreads.items():
        noise = np.random.default_rng([zlib.crc32(name.encode()), seed]).standard_normal(out[name].shape)
        drawn = base * np.exp(spread * noise) if base else spread * noise
        out[name] = jnp.asarray(drawn.astype(out[name].dtype))
    for name, factor in factors.items():
        out[name] = (out[name] * factor).astype(out[name].dtype)
    return out
```

```python
from contextlib import ExitStack

import concourse.bass as bass
from concourse import mybir

F32 = mybir.dt.float32
BF16 = mybir.dt.bfloat16
F16 = mybir.dt.float16
I32 = mybir.dt.int32
U32 = mybir.dt.uint32
ALU = mybir.AluOpType
ACT = mybir.ActivationFunctionType
AX = mybir.AxisListType

P = 128
N, D, E = 3125, 256, 53125
BN = 125
NB = N // BN
HEADS, HD = 8, 32
RELS = 4
COLS = -(-E // P)
PADS = P * COLS - E
CHAINS = 4
CLEN = COLS // CHAINS
TILES = E // P + NB
U = 8
GROUPS = TILES // U
CH = 8
CT = TILES // CH
CU = CT * P
BU = 5
PU = 40
ROW = 264
BIG = 1.0e30
ROUND = 12582912.0
EPS = 1e-5
SCALE = HD ** -0.5
assert TILES % U == 0 and TILES % CH == 0 and TILES % PU == 0 and COLS % CHAINS == 0 and CLEN % 4 == 0
assert TILES * P >= E + NB * (P - 1)


class Count:

    def __init__(self):
        self.n = 0

    def up(self):
        self.n += 1
        return self.n


class Phase(ExitStack):

    number = 0

    def __init__(self, nc):
        super().__init__()
        self.nc, self.sems = nc, []
        Phase.number += 1
        self.number = Phase.number

    def __enter__(self):
        super().__enter__()
        self.callback(self.clear)
        return self

    def clear(self):
        self.nc.clear_and_free_semaphores(self.sems)
        self.nc.all_engine_barrier()

    def sem(self, name):
        self.sems.append(self.nc.alloc_semaphore(f"{name}_{self.number}"))
        return self.sems[-1]

    def block(self):
        return self.enter_context(self.nc.Block())


def bcast(ap, axis, n):
    ap = ap.unsqueeze(axis)
    shape = list(ap.shape)
    shape[axis] = n
    return ap.broadcast_to(shape)


def tile_blocks(nc, eng, table, first):
    return nc.values_load_multi_w_load_instructions(
        table[0:1, bass.ds(first, U)], engines=[eng.engine], min_val=0, max_val=NB - 1)[1]


class Memory:

    def __init__(self, nc, ctx):
        self.nc, self.ctx = nc, ctx
        sb, ps = self.sb, self.ps
        self.x = sb("x_nodes", [BN, NB, D], F32)
        self.acc = sb("acc", [P, CU + 1], F32)
        self.node = sb("node", [P, CU + 1], F32)
        self.edge = sb("edge", [P, 2, TILES * HEADS], F32)
        self.weights = sb("weights", [P, 2, 1280], F32)
        self.bias = sb("bias", [BN, 1280], F32)
        self.rows = sb("rows", [P, U, ROW], F32)
        self.work = sb("work", [P, U, D], F32)
        self.onehot = sb("onehot", [P, U, P], F32)
        self.turned = sb("turned", [P, U, P], F32)
        self.cols = sb("cols", [P, 14, COLS + 4], F32)
        self.src_lane = sb("src_lane", [P, TILES + U], F32)
        self.src_key = sb("src_key", [P, TILES], F32)
        self.src_far = sb("src_far", [P, TILES], I32)
        self.src_block = sb("src_block", [P, TILES], I32)
        self.sort = sb("sort", [P, 1760], F32)
        self.dst_lane = sb("dst_lane", [P, TILES + U], F32)
        self.dst_w = sb("dst_w", [P, TILES + U], F32)
        self.dst_far = sb("dst_far", [P, 2, TILES], I32)
        self.dst_block = sb("dst_block", [P, TILES], I32)
        self.index = sb("index", [P, PU], I32)
        self.ident = sb("ident", [P, P], F32)
        self.lane_of = sb("lane_of", [P, TILES], F32)
        self.lane_h = sb("lane_h", [P, TILES], F16)
        self.ones = sb("ones", [P, P], F32)
        self.ones_b = sb("ones_b", [P, P], BF16)
        self.before = sb("before", [P, P], BF16)
        self.behind = sb("behind", [P, P], BF16)
        self.zeros_b = sb("zeros_b", [P, 512], BF16)
        self.zeros = sb("zeros", [P, P], F32)
        self.stat = sb("stat", [BN, NB, 6], F32)
        self.mv = sb("mv", [BN, NB, 2], F32)
        self.rstd = sb("rstd", [BN, NB], F32)
        self.nbias = sb("nbias", [BN, NB], F32)
        self.a1 = sb("a1", [BN, NB], F32)
        self.a2 = sb("a2", [BN, NB], F32)
        self.dinv = sb("dinv", [BN, NB], F32)
        self.rden = sb("rden", [BN, NB, HEADS], F32)
        self.wa = sb("wa", [BN, 2, D], F32)
        self.ba = sb("ba", [BN, 2], F32)
        self.starts = sb("starts", [P, 2, 32], F32)
        self.small = sb("small", [P, 5, P], F32)
        self.bank = [ps(f"bank{i}", [P, 512], F32) for i in range(8)]
        self.dst_rec = self.acc[:, 0:4 * TILES].rearrange("p (t c) -> p t c", c=4)
        self.sums = self.acc[0:BN, 0:NB * ROW].rearrange("p (b d) -> p b d", b=NB)
        self.nodes = self.node[0:BN, 0:NB * D].rearrange("p (b d) -> p b d", b=NB)
        self.S = self.edge[:, 0, :].rearrange("p (t h) -> p t h", h=HEADS)
        self.S1 = self.edge[:, 0, 0:TILES]
        self.M1 = self.edge[:, 1, 0:TILES]
        self.M = self.edge[:, 1, :].rearrange("p (t h) -> p t h", h=HEADS)
        self.stage = self.edge[:, :, :].rearrange("p a n -> p (a n)")[0:BN, 0:BU * 1280]\
            .rearrange("p (j c) -> p j c", j=BU)

    def sb(self, name, shape, dt):
        return self.ctx.enter_context(self.nc.sbuf_tensor(name, shape, dt))

    def ps(self, name, shape, dt):
        return self.ctx.enter_context(self.nc.psum_tensor(name, shape, dt))


def load_inputs(nc, m, A):
    with Phase(nc) as ctx:
        loaded = ctx.sem("loaded")
        padded = ctx.sem("padded")
        made = ctx.sem("made")
        step = ctx.sem("step")
        block = ctx.block()
        raw = m.cols[:, 8:12, 0:COLS].bitcast(I32)
        full = P - 1
        rest = E - full * COLS

        @block.sync
        def _(eng):
            eng.dma_start(m.x[:, :, :], A["x"].rearrange("(b p) d -> p b d", p=BN)).then_inc(loaded, 16)
            eng.wait_ge(padded, 2)
            for k, name in enumerate(("src", "dst", "edge_type_4", "edge_weight")):
                to = raw[:, k, :] if k < 3 else m.cols[:, 11, 0:COLS]
                eng.dma_start(to[0:full, :], A[name][0:full * COLS].rearrange("(p t) -> p t", p=full)).then_inc(loaded, 16)
                eng.dma_start(to[full:P, 0:rest], A[name][full * COLS:E].rearrange("(p t) -> p t", p=1)).then_inc(loaded, 16)
            eng.wait_ge(loaded, 16 * 9)

        @block.gpsimd
        def _(eng):
            c = Count()
            eng.memset(m.ident[:, :], 0.0).then_inc(made, 1)
            eng.memset(m.ones[:, :], 1.0).then_inc(made, 1)
            eng.memset(m.ones_b[:, :], 1.0).then_inc(made, 1)
            eng.memset(m.zeros_b[:, :], 0.0).then_inc(made, 1)
            eng.memset(m.zeros[:, :], 0.0).then_inc(made, 1)
            eng.iota(m.work[:, 0:2, :].rearrange("p a b -> p (a b)")[:, 0:TILES].bitcast(I32),
                     [[1, TILES]], base=0, channel_multiplier=0).then_inc(made, 1)
            eng.memset(m.before[:, :], 0.0).then_inc(made, 1)
            eng.memset(m.behind[:, :], 0.0).then_inc(made, 1)
            eng.wait_ge(made, 8)
            eng.affine_select(out=m.ident[:, :], in_=m.ident[:, :], compare_op=ALU.not_equal, fill=1.0,
                              base=0, pattern=[[-1, P]], channel_multiplier=1).then_inc(made, 1)
            eng.affine_select(out=m.before[:, :], in_=m.before[:, :], compare_op=ALU.is_ge, fill=1.0,
                              base=0, pattern=[[-1, P]], channel_multiplier=1).then_inc(made, 1)
            eng.affine_select(out=m.behind[:, :], in_=m.behind[:, :], compare_op=ALU.is_ge, fill=1.0,
                              base=-1, pattern=[[1, P]], channel_multiplier=-1).then_inc(made, 1)
            eng.wait_ge(made, 11)

        @block.vector
        def _(eng):
            eng.memset(raw[:, 0:3, :], N).then_inc(padded, 1)
            eng.memset(m.cols[:, 11, :], 0.0).then_inc(padded, 1)
            eng.memset(m.cols[:, 0:8, :], 0.0).then_inc(step, 1)
            eng.memset(m.src_lane[:, :], -1.0).then_inc(step, 1)
            eng.memset(m.dst_lane[:, :], -1.0).then_inc(step, 1)
            eng.memset(m.dst_w[:, :], 0.0).then_inc(step, 1)
            eng.memset(m.rows[:, :, :], 1.0).then_inc(step, 1)
            eng.wait_ge(made, 6)
            iota = m.work[:, 0:2, :].rearrange("p a b -> p (a b)")[:, 0:TILES].bitcast(I32)
            eng.tensor_copy(m.lane_of[:, :], iota).then_inc(step, 1)
            eng.tensor_copy(m.lane_h[:, :], iota).then_inc(step, 1)
            eng.wait_ge(step, 7)


def floor_div(eng, step, c, q, x, d):
    eng.tensor_scalar(q, x, 1.0 / d, 0.5 / d - 0.5, ALU.mult, ALU.add).then_inc(step, 1)
    eng.wait_ge(step, c.up())
    eng.tensor_scalar(q, q, ROUND, ROUND, ALU.add, ALU.subtract).then_inc(step, 1)
    eng.wait_ge(step, c.up())


def remainder(eng, step, c, r, x, q, d):
    eng.scalar_tensor_tensor(out=r, in0=q, scalar=-float(d), in1=x, op0=ALU.mult, op1=ALU.add).then_inc(step, 1)
    eng.wait_ge(step, c.up())


(SRC_LANE, SRC_BLOCK, DST_LANE, DST_BLOCK, PACK0, PACK1, PACK2, WHICH, RAW_SRC, RAW_DST, RAW_TYPE, WEIGHT,
 DST_AT_LANE, DST_AT_TILE) = range(14)


def split_keys(nc, m):
    with Phase(nc) as ctx:
        step = ctx.sem("step")
        block = ctx.block()
        col = [m.cols[:, k, 0:COLS] for k in range(12)]
        t = [m.work[:, 2 * k:2 * k + 2, :].rearrange("p a b -> p (a b)")[:, 0:COLS] for k in range(4)]

        @block.vector
        def _(eng):
            c = Count()
            src, dst, typ, tmp = t

            def do(ins):
                ins.then_inc(step, 1)
                eng.wait_ge(step, c.up())

            do(eng.tensor_copy(src, col[RAW_SRC].bitcast(I32)))
            do(eng.tensor_copy(dst, col[RAW_DST].bitcast(I32)))
            do(eng.tensor_copy(typ, col[RAW_TYPE].bitcast(I32)))
            do(eng.tensor_copy(col[RAW_SRC], src))
            floor_div(eng, step, c, col[SRC_BLOCK], src, BN)
            remainder(eng, step, c, col[SRC_LANE], src, col[SRC_BLOCK], BN)
            floor_div(eng, step, c, col[DST_BLOCK], dst, BN)
            remainder(eng, step, c, col[DST_LANE], dst, col[DST_BLOCK], BN)
            do(eng.scalar_tensor_tensor(out=col[WHICH], in0=typ, scalar=float(N), in1=src,
                                        op0=ALU.mult, op1=ALU.add))
            floor_div(eng, step, c, col[PACK0], src, 16)
            remainder(eng, step, c, tmp, src, col[PACK0], 16)
            floor_div(eng, step, c, typ, dst, 256)
            remainder(eng, step, c, col[PACK2], dst, typ, 256)
            do(eng.scalar_tensor_tensor(out=col[PACK1], in0=tmp, scalar=16.0, in1=typ,
                                        op0=ALU.mult, op1=ALU.add))


def rank(nc, m, key, keys, lane, tile, starts=None):
    with Phase(nc) as ctx:
        sem = ctx.sem
        step, ahead, free = sem("step"), sem("ahead"), sem("free")
        seeds = sem("seeds")
        ready, ranked, placed = sem("ready"), sem("ranked"), sem("placed")
        n = CHAINS * keys
        oh = m.sort[:, 0:2 * n].bitcast(BF16).rearrange("p (u c k) -> p u c k", u=4, c=CHAINS)
        total = m.sort[:, 2 * n:3 * n].rearrange("p (c k) -> p c k", c=CHAINS)
        turned = m.turned[:, :, :].rearrange("p a b -> p (a b)")
        junk = turned[:, 0:n].rearrange("p (c k) -> p c k", c=CHAINS)
        base = turned[:, n:2 * n].rearrange("p (c k) -> p c k", c=CHAINS)
        whole = m.small[:, 0:2, 0:keys]
        block = ctx.block()
        bank = [m.bank[c][:, 0:keys] for c in range(CHAINS)]

        @block.tensor
        def _(eng):
            for c in range(CHAINS):
                eng.matmul(bank[c], m.ones_b[:, :], m.zeros_b[:, 0:keys], start=True, stop=False, skip_group_check=True)
            with eng.Fori(0, CLEN // 4) as i:
                for u in range(4):
                    for c in range(CHAINS):
                        eng.wait_ge(ahead, i * 16 + (4 * u + c + 1))
                        eng.matmul(bank[c], m.ones_b[:, :], oh[:, u, c, :], start=False, stop=True,
                                   skip_group_check=True).then_inc(free, 1)
            eng.wait_ge(seeds, 1)
            for c in range(CHAINS):
                eng.matmul(bank[c], m.ones[0:1, :], base[0:1, c, :], start=True, stop=False,
                           skip_group_check=True)
            for c in range(CHAINS):
                eng.wait_ge(ready, c + 1)
                eng.matmul(bank[c], m.before[:, :], oh[:, 0, c, :], start=False, stop=True,
                           skip_group_check=True).then_inc(placed, 1)
            with eng.Fori(0, CLEN // 4) as i:
                for u in range(4):
                    for c in range(CHAINS):
                        eng.wait_ge(ranked, i * 16 + (4 * u + c + 1))
                        eng.matmul(bank[c], m.behind[:, :], oh[:, u, c, :], start=False, stop=True,
                                   skip_group_check=True)
                        eng.wait_ge(ready, i * 16 + (4 * u + c + 5))
                        eng.matmul(bank[c], m.before[:, :], oh[:, (u + 1) % 4, c, :], start=False, stop=True,
                                   skip_group_check=True).then_inc(placed, 1)

        @block.vector
        def _(eng):
            c_ = Count()

            def one_hot(u, c, column, signal):
                eng.tensor_scalar(oh[:, u, c, :], m.lane_h[:, 0:keys], key[:, bass.ds(column, 1)], None,
                                  ALU.is_equal).then_inc(signal, 1)

            for u in range(4):
                for c in range(CHAINS):
                    one_hot(u, c, c * CLEN + u, ahead)
            with eng.Fori(1, CLEN // 4) as i:
                for u in range(4):
                    for c in range(CHAINS):
                        eng.wait_ge(free, i * 16 + (4 * u + c + 1 - 16))
                        one_hot(u, c, i * 4 + (c * CLEN + u), ahead)
            eng.wait_ge(free, CLEN * CHAINS)
            for c in range(CHAINS):
                eng.tensor_copy(total[:, c, :], bank[c]).then_inc(step, 1)
                c_.up()
            eng.wait_ge(step, c_.n)
            eng.tensor_copy(base[:, 0, :], total[:, 0, :]).then_inc(step, 1)
            eng.wait_ge(step, c_.up())
            for c in range(1, CHAINS):
                eng.tensor_tensor(base[:, 0, :], base[:, 0, :], total[:, c, :], ALU.add).then_inc(step, 1)
                eng.wait_ge(step, c_.up())
            if starts is not None:
                floor_div(eng, step, c_, whole[:, 0, :], base[:, 0, :], P)
                remainder(eng, step, c_, whole[:, 1, :], base[:, 0, :], whole[:, 0, :], P)
                eng.tensor_scalar(whole[:, 1, :], whole[:, 1, :], 0.0, None, ALU.is_gt).then_inc(step, 1)
                eng.wait_ge(step, c_.up())
                eng.tensor_tensor(base[:, 0, :], whole[:, 0, :], whole[:, 1, :], ALU.add).then_inc(step, 1)
                eng.wait_ge(step, c_.up())
            eng.tensor_tensor_scan(whole[:, 0, :], base[:, 0, :], m.zeros[:, 0:keys], 0.0, ALU.add, ALU.add).then_inc(step, 1)
            eng.wait_ge(step, c_.up())
            eng.tensor_tensor(whole[:, 1, :], whole[:, 0, :], base[:, 0, :], ALU.subtract).then_inc(step, 1)
            eng.wait_ge(step, c_.up())
            if starts is not None:
                eng.memset(whole[:, 1, keys - 1:keys], float(TILES)).then_inc(step, 1)
                eng.wait_ge(step, c_.up())
                eng.tensor_copy(starts[:, 0:keys], whole[:, 1, :]).then_inc(step, 1)
                eng.wait_ge(step, c_.up())
            eng.tensor_scalar(base[:, 0, :], whole[:, 1, :], float(P if starts is not None else 1), None,
                              ALU.mult).then_inc(step, 1)
            eng.wait_ge(step, c_.up())
            for c in range(1, CHAINS):
                eng.tensor_tensor(base[:, c, :], base[:, c - 1, :], total[:, c - 1, :], ALU.add).then_inc(step, 1)
                eng.wait_ge(step, c_.up())
            eng.sem_inc(seeds, 1)
            for u in range(2):
                for c in range(CHAINS):
                    one_hot(u, c, c * CLEN + u, ready)
            with eng.Fori(0, CLEN // 4) as i:
                for u in range(4):
                    for c in range(CHAINS):
                        eng.wait_ge(placed, i * 16 + (4 * u + c + 1))
                        column = i * 4 + (c * CLEN + u)
                        eng.scalar_tensor_tensor(out=junk[:, c, :], in0=bank[c], scalar=1.0, in1=oh[:, u, c, :],
                                                 op0=ALU.mult, op1=ALU.mult,
                                                 accum_out=lane[:, bass.ds(column, 1)]).then_inc(ranked, 1)
                        one_hot((u + 2) % 4, c, i * 4 + (c * CLEN + u + 2), ready)
            eng.wait_ge(ranked, CLEN * CHAINS)
            floor_div(eng, step, c_, tile[:, 0:COLS], lane[:, 0:COLS], P)
            remainder(eng, step, c_, lane[:, 0:COLS], lane[:, 0:COLS], tile[:, 0:COLS], P)


def permute(nc, m, values, lane, tile, tiles, out):
    with Phase(nc) as ctx:
        sem = ctx.sem
        ready, moved, step = sem("ready"), sem("moved"), sem("step")
        at_tile = m.sort[:, 0:2 * tiles].bitcast(BF16).rearrange("p (u t) -> p u t", u=4)
        at_lane = m.sort[:, 2 * tiles:2 * tiles + 6 * P].bitcast(BF16).rearrange("p (u v q) -> p u v q", u=4, v=3)
        block = ctx.block()

        @block.tensor
        def _(eng):
            for v in range(3):
                eng.matmul(m.bank[v][:, 0:tiles], m.ones_b[:, :], m.zeros_b[:, 0:tiles], start=True, stop=False,
                           skip_group_check=True)
            with eng.Fori(0, COLS // 4) as i:
                for u in range(4):
                    eng.wait_ge(ready, i * 4 + (u + 1))
                    for v in range(3):
                        mm = eng.matmul(m.bank[v][:, 0:tiles], at_lane[:, u, v, :], at_tile[:, u, :],
                                        start=False, stop=True, skip_group_check=True)
                    mm.then_inc(moved, 1)

        @block.vector
        def _(eng):
            def one_hots(u, column):
                eng.tensor_scalar(at_tile[:, u, :], m.lane_h[:, 0:tiles], tile[:, bass.ds(column, 1)], None,
                                  ALU.is_equal)
                for v in range(3):
                    last = eng.tensor_scalar(at_lane[:, u, v, :], m.lane_h[:, 0:P], lane[:, bass.ds(column, 1)],
                                             values[v][:, bass.ds(column, 1)], ALU.is_equal, ALU.mult)
                last.then_inc(ready, 1)

            for u in range(4):
                one_hots(u, u)
            with eng.Fori(1, COLS // 4) as i:
                for u in range(4):
                    eng.wait_ge(moved, i * 4 + (u + 1 - 4))
                    one_hots(u, i * 4 + u)
            eng.wait_ge(moved, COLS)
            for v in range(3):
                eng.tensor_copy(out[v], m.bank[v][:, 0:tiles]).then_inc(step, 1)
            eng.wait_ge(step, 3)


def between_passes(nc, m):
    with Phase(nc) as ctx:
        step = ctx.sem("step")
        block = ctx.block()
        col = [m.cols[:, k, 0:COLS] for k in range(12)]
        src = m.work[:, 0:2, :].rearrange("p a b -> p (a b)")[:, 0:COLS]

        @block.vector
        def _(eng):
            c = Count()
            floor_div(eng, step, c, col[WHICH + 1], col[PACK1], 16)
            eng.scalar_tensor_tensor(out=src, in0=col[PACK0], scalar=16.0, in1=col[WHICH + 1],
                                     op0=ALU.mult, op1=ALU.add).then_inc(step, 1)
            eng.wait_ge(step, c.up())
            remainder(eng, step, c, col[PACK1], col[PACK1], col[WHICH + 1], 16)
            floor_div(eng, step, c, col[SRC_BLOCK], src, BN)
            remainder(eng, step, c, col[PACK0], src, col[SRC_BLOCK], BN)
            eng.tensor_scalar(col[PACK0], col[PACK0], 1.0, None, ALU.add).then_inc(step, 1)
            eng.wait_ge(step, c.up())


def source_order(nc, m, got):
    with Phase(nc) as ctx:
        step = ctx.sem("step")
        block = ctx.block()
        tmp = m.acc[:, 0:TILES * (NB - 1) // 2].bitcast(BF16).rearrange("p (t b) -> p t b", b=NB - 1)

        @block.vector
        def _(eng):
            c = Count()
            def kept(ap):
                return ap.rearrange("p (t c) -> p c t", c=CH)

            def of(ap):
                return ap.rearrange("p (c t) -> p c t", c=CH)

            eng.tensor_scalar(kept(m.src_lane[:, 0:TILES]), of(got[0]), -1.0, None, ALU.add).then_inc(step, 1)
            eng.scalar_tensor_tensor(out=got[1], in0=got[1], scalar=256.0, in1=got[2],
                                     op0=ALU.mult, op1=ALU.add).then_inc(step, 1)
            c.up(), c.up()
            eng.wait_ge(step, c.n)
            eng.tensor_copy(kept(m.src_far[:, :]), of(got[1])).then_inc(step, 1)
            eng.wait_ge(step, c.up())
            eng.tensor_tensor(tmp, bcast(m.lane_of[:, :], 2, NB - 1), bcast(m.starts[:, 0, 1:NB], 1, TILES), ALU.is_ge).then_inc(step, 1)
            eng.wait_ge(step, c.up())
            eng.tensor_reduce(got[1], tmp, AX.X, ALU.add).then_inc(step, 1)
            eng.wait_ge(step, c.up())
            eng.tensor_copy(kept(m.src_block[:, :]), of(got[1])).then_inc(step, 1)
            eng.scalar_tensor_tensor(out=kept(m.src_key[:, :]), in0=of(got[1]), scalar=float(BN + 1), in1=of(got[0]),
                                     op0=ALU.mult, op1=ALU.add).then_inc(step, 1)
            c.up(), c.up()
            eng.wait_ge(step, c.n)


def target_order(nc, m, table):
    with Phase(nc) as ctx:
        sem = ctx.sem
        step, blank, filled, staged, index_made = sem("step"), sem("blank"), sem("filled"), sem("staged"), sem("index_made")
        landed = [sem(f"landed{j}") for j in range(U)]
        back, issued = sem("back"), sem("issued")
        block = ctx.block()
        blanks = m.node[:, 0:4 * (TILES + 1)].rearrange("p (t c) -> p t c", c=4)
        place = m.node[:, 2000:2000 + COLS].bitcast(I32)
        place_f = m.node[:, 2500:2500 + COLS]
        tmp = m.node[:, 3000:3000 + TILES * (NB - 1) // 4].bitcast(BF16)\
            .rearrange("p (t b) -> p t b", b=NB - 1)
        block_f = m.small[:, 0:4, :].rearrange("p a b -> p (a b)")[:, 0:TILES]
        rec = m.rows[:, :, 0:4]
        idx = m.index[:, 0:U]

        @block.vector
        def _(eng):
            c = Count()
            eng.memset(blanks, 0.0).then_inc(step, 1)
            eng.wait_ge(step, c.up())
            eng.memset(blanks[:, :, 0:1], -1.0).then_inc(blank, 1)
            eng.scalar_tensor_tensor(out=place_f, in0=m.cols[:, DST_AT_LANE, 0:COLS], scalar=float(TILES + 1),
                                     in1=m.cols[:, DST_AT_TILE, 0:COLS], op0=ALU.mult, op1=ALU.add).then_inc(step, 1)
            eng.wait_ge(step, c.up())
            eng.tensor_copy(place, place_f).then_inc(index_made, 1)

        @block.scalar
        def _(eng):
            eng.wait_ge(index_made, 1)
            def stage_columns(i, later):
                for j in range(U):
                    if later:
                        eng.wait_ge(landed[j], i * 16)
                    column = i * U + j
                    eng.activation(idx[:, j:j + 1], place[:, bass.ds(column, 1)], ACT.Copy)
                    for k, what in enumerate((DST_LANE, RAW_SRC, WHICH, WEIGHT)):
                        last = eng.activation(rec[:, j, k:k + 1], m.cols[:, what, bass.ds(column, 1)], ACT.Copy)
                    last.then_inc(staged, 1)

            stage_columns(0, False)
            with eng.Fori(1, COLS // U) as i:
                stage_columns(i, True)

        @block.gpsimd
        def _(eng):
            eng.wait_ge(filled, 16)
            with eng.Fori(0, COLS // U) as i:
                for j in range(U):
                    eng.wait_ge(staged, i * U + (j + 1))
                    eng.sem_inc(issued, 1)
                    eng.indirect_dma_start(out=table, out_offset=bass.IndirectOffsetOnAxis(ap=idx[:, j:j + 1].bitcast(U32), axis=0),
                                           in_=rec[:, j, :], in_offset=None).then_inc(landed[j], 16)

        @block.sync
        def _(eng):
            eng.wait_ge(blank, 1)
            eng.dma_start(table.rearrange("(p t) c -> p t c", p=P), blanks).then_inc(filled, 16)
            for j in range(U):
                eng.wait_ge(landed[j], 16 * (COLS // U))
            eng.dma_start(m.dst_rec[:, :, :], table.rearrange("(p t) c -> p t c", p=P)[:, 0:TILES, :]).then_inc(back, 16)
            eng.wait_ge(back, 16)

    with Phase(nc) as ctx:
        step = ctx.sem("step")
        block = ctx.block()
        half = TILES // 2

        @block.vector
        def _(eng):
            c = Count()
            eng.tensor_copy(m.dst_lane[:, 0:TILES], m.dst_rec[:, :, 0]).then_inc(step, 1)
            eng.tensor_copy(m.dst_far[:, 1, :], m.dst_rec[:, :, 1]).then_inc(step, 1)
            eng.tensor_copy(m.dst_far[:, 0, :], m.dst_rec[:, :, 2]).then_inc(step, 1)
            eng.tensor_copy(m.dst_w[:, 0:TILES], m.dst_rec[:, :, 3]).then_inc(step, 1)
            for _k in range(4):
                c.up()
            eng.wait_ge(step, c.n)
            for h in range(2):
                eng.tensor_tensor(tmp, bcast(m.lane_of[:, h * half:(h + 1) * half], 2, NB - 1),
                                  bcast(m.starts[:, 1, 1:NB], 1, half), ALU.is_ge).then_inc(step, 1)
                eng.wait_ge(step, c.up())
                eng.tensor_reduce(block_f[:, h * half:(h + 1) * half], tmp, AX.X, ALU.add).then_inc(step, 1)
                eng.wait_ge(step, c.up())
            eng.tensor_copy(m.dst_block[:, :], block_f).then_inc(step, 1)
            eng.wait_ge(step, c.up())


def norm_stats(eng, step, c, m):
    for b in range(NB):
        eng.bn_stats(m.stat[:, b, :], m.x[:, b, :]).then_inc(step, 1)
        c.up()
    eng.wait_ge(step, c.n)
    for b in range(NB):
        eng.bn_aggr(m.mv[:, b, :], m.stat[:, b, :]).then_inc(step, 1)
        c.up()
    eng.wait_ge(step, c.n)
    eng.tensor_scalar(m.rstd[:, :], m.mv[:, :, 1], EPS, None, ALU.add).then_inc(step, 1)
    eng.wait_ge(step, c.up())


def project(nc, m, groups, finish, loads, divide=False, store=None, stored=0, after=None):
    with Phase(nc) as ctx:
        sem = ctx.sem
        step, var_ready, root_ready, scale_ready = sem("step"), sem("var_ready"), sem("root_ready"), sem("scale_ready")
        loaded, h_ready, turned, copied = sem("loaded"), sem("h_ready"), sem("turned"), sem("copied")
        summed, taken, noted = sem("summed"), sem("taken"), sem("noted")
        out_done = [sem(f"out_done{j}") for j in range(BU)]
        block = ctx.block()
        G = len(groups)
        TURNS = NB // BU
        h = m.work[0:BN, 0:BU, :]
        hT = [t[:, :, :].rearrange("p a b -> p (a b)")[:, 0:BU * BN].rearrange("p (j n) -> p j n", j=BU)
              for t in (m.turned, m.onehot)]

        def turned_psum(j, k):
            return m.bank[j % 3][:, k * P:k * P + BN]

        def out_psum(j, g):
            a, z = groups[g]
            return m.bank[3 + (j * G + g) % BU][0:BN, 0:z - a]

        @block.sync
        def _(eng):
            for to, of in loads:
                eng.dma_start(to, of).then_inc(loaded, 16)
            if store is not None:
                with eng.Fori(0, TURNS) as i:
                    for j in range(BU):
                        eng.wait_ge(taken, i * (BU * G) + (BU + j * G + G))
                        for to, of in store(i * BU + j, j):
                            eng.dma_start(to, of).then_inc(out_done[j], 16)
                for j in range(BU):
                    eng.wait_ge(out_done[j], 16 * stored * TURNS)
            eng.wait_ge(loaded, 16 * len(loads))

        @block.scalar
        def _(eng):
            if not divide:
                eng.wait_ge(var_ready, 1)
                eng.activation(m.rstd[:, :], m.rstd[:, :], ACT.Sqrt).then_inc(root_ready, 1)
                eng.wait_ge(scale_ready, 1)
            with eng.Fori(0, TURNS) as i:
                if not divide:
                    for j in range(BU):
                        b = i * BU + j
                        eng.wait_ge(turned, i * BU + (j + 1))
                        eng.activation(h[:, j, :], m.x[:, bass.ds(b, 1), :].rearrange("p a d -> p (a d)"), ACT.Relu,
                                       bias=m.nbias[:, bass.ds(b, 1)], scale=m.rstd[:, bass.ds(b, 1)]).then_inc(h_ready, 1)
                for j in range(BU):
                    eng.wait_ge(turned, i * BU + (BU + j + 1))
                    for k in range(2):
                        cp = eng.activation(hT[k][:, j, :], turned_psum(j, k), ACT.Copy)
                    cp.then_inc(copied, 1)

        @block.tensor
        def _(eng):
            eng.sem_inc(turned, BU)
            eng.wait_ge(loaded, 16 * len(loads))
            with eng.Fori(0, TURNS) as i:
                for j in range(BU):
                    eng.wait_ge(h_ready, i * BU + (j + 1))
                    if j >= 3:
                        eng.wait_ge(copied, i * BU + (j - 2))
                    for k in range(2):
                        tr = eng.transpose(turned_psum(j, k), h[:, j, k * P:(k + 1) * P], m.ident[0:BN, 0:BN])
                    tr.then_inc(turned, 1)
                for j in range(BU):
                    eng.wait_ge(copied, i * BU + (j + 1))
                    for g, (a, z) in enumerate(groups):
                        eng.wait_ge(taken, i * (BU * G) + (j * G + g + 1))
                        for k in range(2):
                            mm = eng.matmul(out_psum(j, g), hT[k][:, j, :], m.weights[:, k, a:z],
                                            start=(k == 0), stop=(k == 1))
                        mm.then_inc(summed, 1)

        @block.vector
        def _(eng):
            c = Count()
            eng.sem_inc(taken, BU)
            if divide:
                eng.tensor_scalar(m.rden[:, :, :], m.sums[:, :, D:D + HEADS], 0.5, None, ALU.max).then_inc(step, 1)
                eng.wait_ge(step, c.up())
                eng.reciprocal(m.rden[:, :, :], m.rden[:, :, :]).then_inc(step, 1)
                eng.wait_ge(step, c.up())
            else:
                norm_stats(eng, step, c, m)
                eng.sem_inc(var_ready, 1)
                eng.wait_ge(root_ready, 1)
                eng.reciprocal(m.rstd[:, :], m.rstd[:, :]).then_inc(step, 1)
                eng.wait_ge(step, c.up())
                eng.scalar_tensor_tensor(out=m.nbias[:, :], in0=m.mv[:, :, 0], scalar=-1.0, in1=m.rstd[:, :],
                                         op0=ALU.mult, op1=ALU.mult).then_inc(scale_ready, 1)
            eng.wait_ge(loaded, 16 * len(loads))
            def turn_of_blocks(i, later):
                if divide:
                    for j in range(BU):
                        b = i * BU + j
                        eng.wait_ge(turned, i * BU + (j + 1))
                        eng.tensor_tensor(h[:, j, :].rearrange("p (h d) -> p h d", h=HEADS),
                                          m.sums[:, bass.ds(b, 1), 0:D].rearrange("p a (h d) -> p (a h) d", h=HEADS),
                                          bcast(m.rden[:, bass.ds(b, 1), :].rearrange("p a h -> p (a h)"), 2, HD),
                                          ALU.mult).then_inc(h_ready, 1)
                if after is not None and later:
                    eng.wait_ge(noted, i * BU)
                for j in range(BU):
                    b = i * BU + j
                    if store is not None and later:
                        eng.wait_ge(out_done[j], i * (16 * stored))
                    for g in range(G):
                        eng.wait_ge(summed, i * (BU * G) + (j * G + g + 1))
                        finish(eng, j, b, g, out_psum(j, g)).then_inc(taken, 1)
                if after is not None:
                    for j in range(BU):
                        eng.wait_ge(taken, i * (BU * G) + (BU + j * G + G))
                        after(eng, j, i * BU + j).then_inc(noted, 1)

            turn_of_blocks(0, False)
            with eng.Fori(1, TURNS) as i:
                turn_of_blocks(i, True)


def gather_tiles(eng, nc, m, sems, index, table, width, used, copied, issued):
    with eng.Fori(0, TILES // PU) as q:
        for u in range(PU):
            if u % (PU // 2) == 0:
                eng.tensor_copy(m.index[:, u:u + PU // 2], index[:, bass.ds(q * PU + u, PU // 2)]).then_inc(copied, 1)
                eng.wait_ge(copied, q * 2 + (u * 2 // PU + 1))
            eng.wait_ge(used, q * PU + (u + 1))
            eng.sem_inc(issued, 1)
            eng.indirect_dma_start(out=m.rows[:, u % U, 0:width], out_offset=None, in_=table,
                                   in_offset=bass.IndirectOffsetOnAxis(ap=m.index[:, u:u + 1].bitcast(U32), axis=0))\
               .then_inc(sems[u % U], 16)


def edge_scores(nc, m, index, table, width, additive):
    with Phase(nc) as ctx:
        sem = ctx.sem
        gathered = [sem(f"gathered{j}") for j in range(U)]
        used, copied, issued = sem("used"), sem("copied"), sem("issued")
        hot, turned, evacuated, near, mixed, step = sem("hot"), sem("turned"), sem("evacuated"), sem("near"), sem("mixed"), sem("step")
        block = ctx.block()
        width_near = 1 if additive else D

        def turned_psum(j):
            return m.bank[j % 4][0:BN, 0:P]

        def near_psum(j):
            return m.bank[4 + j % 4][:, 0:width_near]

        @block.gpsimd
        def _(eng):
            gather_tiles(eng, nc, m, gathered, index, table, width, used, copied, issued)

        @block.scalar
        def _(eng):
            with eng.Fori(0, GROUPS) as g:
                for j in range(U):
                    eng.wait_ge(turned, g * U + (j + 1))
                    eng.activation(m.turned[0:BN, j, :], turned_psum(j), ACT.Copy).then_inc(evacuated, 1)

        @block.tensor
        def _(eng):
            def turn(j, count, copies):
                eng.wait_ge(hot, count)
                if copies is not None:
                    eng.wait_ge(evacuated, copies)
                eng.transpose(turned_psum(j), m.onehot[:, j, 0:BN], m.ident[:, :]).then_inc(turned, 1)

            def take_near(g, j, b):
                eng.wait_ge(evacuated, g * U + (j + 1))
                eng.wait_ge(used, g * U + (j + 5))
                of = m.a1[:, bass.ds(b, 1)] if additive else \
                    m.nodes[:, bass.ds(b, 1), :].rearrange("p a d -> p (a d)")
                eng.matmul(near_psum(j), m.turned[0:BN, j, :], of, start=True, stop=True).then_inc(near, 1)

            for j in range(U):
                turn(j, j + 1, j - 3 if j >= 4 else None)
            with eng.Fori(0, GROUPS - 1) as g:
                blocks = tile_blocks(nc, eng, m.src_block, g * U)
                for j in range(U):
                    take_near(g, j, blocks[j])
                    turn(j, g * U + (U + j + 1), g * U + (j + 5))
            blocks = tile_blocks(nc, eng, m.src_block, TILES - U)
            for j in range(U):
                take_near(GROUPS - 1, j, blocks[j])

        @block.vector
        def _(eng):
            eng.sem_inc(used, U)

            def one_hot(j, tile):
                eng.tensor_scalar(m.onehot[:, j, 0:BN], m.lane_of[:, 0:BN], m.src_lane[:, bass.ds(tile, 1)], None,
                                  ALU.is_equal).then_inc(hot, 1)

            def mix(g, j):
                eng.wait_ge(near, g * U + (j + 1))
                eng.wait_ge(gathered[j], g * 16 + 16)
                if additive:
                    eng.tensor_tensor(m.S1[:, bass.ds(g * U + j, 1)], near_psum(j), m.rows[:, j, 0:1], ALU.add).then_inc(used, 1)
                else:
                    eng.tensor_tensor(m.work[:, j, :], near_psum(j), m.rows[:, j, 0:D], ALU.mult).then_inc(used, 1)

            def heads(g, j):
                eng.wait_ge(used, g * U + (U + j + 1))
                eng.tensor_reduce(m.S[:, bass.ds(g * U + j, 1), :].rearrange("p a h -> p (a h)"),
                                  m.work[:, j, :].rearrange("p (h d) -> p h d", h=HEADS), AX.X, ALU.add).then_inc(mixed, 1)

            def group(g, more):
                for j in range(U):
                    if more:
                        eng.wait_ge(turned, g * U + (j + 1))
                        one_hot(j, g * U + (U + j))
                    mix(g, j)
                    if j and not additive:
                        heads(g, j - 1)
                if not additive:
                    heads(g, U - 1)

            for j in range(U):
                one_hot(j, j)
            with eng.Fori(0, GROUPS - 1) as g:
                group(g, True)
            group(GROUPS - 1, False)
            if additive:
                eng.wait_ge(used, TILES + U)
                eng.scalar_tensor_tensor(out=m.S1[:, :], in0=m.S1[:, :], scalar=0.01, in1=m.S1[:, :],
                                         op0=ALU.mult, op1=ALU.max).then_inc(step, 1)
                eng.wait_ge(step, 1)


def softmax_weights(nc, m, H, scores, maxima, scale):
    L = CH * H
    with Phase(nc) as ctx:
        sem = ctx.sem
        keys, turned, evacuated, scored, stepped = sem("keys"), sem("turned"), sem("evacuated"), sem("scored"), sem("stepped")
        step, ends, ends_turned, carried, carried_turned = sem("step"), sem("ends"), sem("ends_turned"), sem("carried"), sem("carried_turned")
        done, subtracted = sem("done"), sem("subtracted")
        block = ctx.block()
        wide_key = maxima
        steps = m.acc[0:L, 0:CU + 1]
        vals = m.node[0:L, 0:CU]
        col = m.small[0:L, 4, 0:8]
        row = m.small[0:1, 0:4, :]

        def turn_in(eng, of, j, n):
            return eng.transpose(m.bank[n % 4][0:L, 0:P], of[:, j * CH:(j + 1) * CH, :].rearrange("p c h -> p (c h)"),
                                 m.ident[:, :])

        @block.tensor
        def _(eng):
            eng.wait_ge(keys, 1)
            for j in range(CT):
                if j >= 4:
                    eng.wait_ge(evacuated, j - 3)
                turn_in(eng, wide_key, j, j).then_inc(turned, 1)
            for j in range(CT):
                eng.wait_ge(evacuated, CT + j - 3)
                turn_in(eng, scores, j, CT + j).then_inc(turned, 1)
            for way in range(2):
                eng.wait_ge(ends, way + 1)
                for k in range(4):
                    tr = eng.transpose(m.bank[4 + k][0:1, 0:L], col[:, (0, 1, 2, 3 + way)[k]:(0, 1, 2, 3 + way)[k] + 1],
                                       m.ident[0:L, 0:L])
                tr.then_inc(ends_turned, 1)
                eng.wait_ge(carried, way + 1)
                eng.transpose(m.bank[4][0:L, 0:1], row[:, 3, 0:L], m.ident[0:1, 0:1]).then_inc(carried_turned, 1)
            eng.wait_ge(scored, 1)
            for j in range(CT):
                eng.wait_ge(evacuated, 2 * CT + j - 3)
                eng.transpose(m.bank[(2 * CT + j) % 4][:, 0:L], vals[:, j * P:(j + 1) * P], m.ident[0:L, 0:L]).then_inc(turned, 1)

        @block.scalar
        def _(eng):
            for j in range(CT):
                eng.wait_ge(turned, j + 1)
                eng.activation(vals[:, j * P:(j + 1) * P], m.bank[j % 4][0:L, 0:P], ACT.Copy).then_inc(evacuated, 1)
            eng.wait_ge(stepped, 1)
            for j in range(CT):
                eng.wait_ge(turned, CT + j + 1)
                eng.activation(vals[:, j * P:(j + 1) * P], m.bank[(CT + j) % 4][0:L, 0:P], ACT.Copy).then_inc(evacuated, 1)
            for j in range(CT):
                eng.wait_ge(turned, 2 * CT + j + 1)
                eng.activation(maxima[:, j * CH:(j + 1) * CH, :], m.bank[(2 * CT + j) % 4][:, 0:L].rearrange("p (c h) -> p c h", c=CH),
                               ACT.Copy).then_inc(evacuated, 1)
            eng.wait_ge(subtracted, 1)
            eng.activation(scores, scores, ACT.Exp, scale=scale).then_inc(done, 1)

        @block.vector
        def _(eng):
            c = Count()

            def do(ins):
                ins.then_inc(step, 1)
                eng.wait_ge(step, c.up())

            eng.tensor_copy(wide_key, bcast(m.src_key[:, :], 2, H)).then_inc(keys, 1)
            eng.wait_ge(evacuated, CT)
            do(eng.memset(steps, 0.0))
            do(eng.tensor_tensor(steps[:, 1:CU], vals[:, 1:CU], vals[:, 0:CU - 1], ALU.not_equal))
            do(eng.tensor_scalar(steps[:, 1:CU], steps[:, 1:CU], -BIG, None, ALU.mult))
            do(eng.tensor_copy(col[:, 0:1], vals[:, 0:1]))
            do(eng.tensor_copy(col[:, 1:2], vals[:, CU - 1:CU]))
            do(eng.tensor_reduce(col[:, 2:3], steps[:, 0:CU], AX.X, ALU.min))
            eng.sem_inc(stepped, 1)
            eng.wait_ge(evacuated, 2 * CT)
            for way in range(2):
                if way == 0:
                    do(eng.tensor_tensor_scan(vals, steps[:, 0:CU], vals, -BIG, ALU.add, ALU.max))
                    do(eng.tensor_copy(col[:, 3:4], vals[:, CU - 1:CU]))
                else:
                    do(eng.tensor_tensor_scan(vals[:, ::-1], steps[:, CU:0:-1], vals[:, ::-1], -BIG, ALU.add, ALU.max))
                    do(eng.tensor_copy(col[:, 4:5], vals[:, 0:1]))
                eng.sem_inc(ends, 1)
                eng.wait_ge(ends_turned, way + 1)
                first, final, alone, end = [m.bank[4 + k][0:1, 0:L].rearrange("p (c h) -> p h c", c=CH) for k in range(4)]
                a = row[:, 0, 0:L].rearrange("p (h c) -> p h c", h=H)
                b = row[:, 1, 0:L].rearrange("p (h c) -> p h c", h=H)
                s = row[:, 2, 0:L].rearrange("p (h c) -> p h c", h=H)
                firsts = row[:, 3, 0:L].rearrange("p (h c) -> p h c", h=H)
                do(eng.memset(row[:, 0, 0:L], 1.0))
                do(eng.tensor_copy(firsts, first))
                do(eng.tensor_tensor(a[:, :, 1:CH], firsts[:, :, 1:CH], final[:, :, 0:CH - 1], ALU.not_equal))
                do(eng.tensor_scalar(row[:, 0, 0:L], row[:, 0, 0:L], -BIG, None, ALU.mult))
                if way == 0:
                    do(eng.tensor_copy(b, a))
                    do(eng.tensor_tensor(b[:, :, 1:CH], a[:, :, 1:CH], end[:, :, 0:CH - 1], ALU.add))
                    do(eng.tensor_tensor(a[:, :, 1:CH], a[:, :, 1:CH], alone[:, :, 0:CH - 1], ALU.add))
                    do(eng.tensor_tensor_scan(row[:, 2, 0:L], row[:, 0, 0:L], row[:, 1, 0:L], -BIG, ALU.add, ALU.max))
                else:
                    do(eng.memset(row[:, 1, 0:L], -BIG))
                    do(eng.tensor_tensor(b[:, :, 0:CH - 1], a[:, :, 1:CH], end[:, :, 1:CH], ALU.add))
                    do(eng.memset(row[:, 3, 0:L], -BIG))
                    do(eng.tensor_tensor(firsts[:, :, 0:CH - 1], a[:, :, 1:CH], alone[:, :, 1:CH], ALU.add))
                    do(eng.tensor_tensor_scan(row[:, 2, 0:L][:, ::-1], row[:, 3, 0:L][:, ::-1], row[:, 1, 0:L][:, ::-1],
                                              -BIG, ALU.add, ALU.max))
                do(eng.tensor_copy(row[:, 3, 0:L].rearrange("p (c h) -> p h c", c=CH), s))
                eng.sem_inc(carried, 1)
                eng.wait_ge(carried_turned, way + 1)
                do(eng.tensor_copy(col[:, 5 + way:6 + way], m.bank[4][0:L, 0:1]))
                if way == 0:
                    do(eng.tensor_tensor_scan(vals, steps[:, 0:CU], vals, col[:, 5:6], ALU.add, ALU.max))
                else:
                    do(eng.tensor_tensor_scan(vals[:, ::-1], steps[:, CU:0:-1], vals[:, ::-1], col[:, 6:7], ALU.add, ALU.max))
            eng.sem_inc(scored, 1)
            eng.wait_ge(evacuated, 3 * CT)
            eng.tensor_tensor(scores, scores, maxima, ALU.subtract).then_inc(subtracted, 1)
            eng.wait_ge(done, 1)


def sum_over_edges(nc, m, near_lane, weight, tile_block, index, table, width, own=None, heads=False):
    with Phase(nc) as ctx:
        sem = ctx.sem
        gathered = [sem(f"gathered{j}") for j in range(U)]
        used, copied, issued, hot, added, owned = sem("used"), sem("copied"), sem("issued"), sem("hot"), sem("added"), sem("owned")
        block = ctx.block()

        def psum(j):
            return m.bank[j][0:BN, 0:width]

        @block.gpsimd
        def _(eng):
            gather_tiles(eng, nc, m, gathered, index, table, D, used, copied, issued)

        @block.scalar
        def _(eng):
            with eng.Fori(0, GROUPS) as g:
                for j in range(U):
                    if heads or own is not None:
                        eng.wait_ge(used, g * U + (j + 1))
                        if heads:
                            eng.activation(m.rows[:, j, D:D + HEADS], m.S[:, bass.ds(g * U + j, 1), :].rearrange("p a h -> p (a h)"),
                                           ACT.Copy).then_inc(owned, 1)
                        else:
                            eng.activation(m.rows[:, j, D + 1:D + 2], own[:, bass.ds(g * U + j, 1)], ACT.Copy).then_inc(owned, 1)

        @block.tensor
        def _(eng):
            eng.sem_inc(used, U)
            with eng.Fori(0, GROUPS) as g:
                for j in range(U):
                    eng.wait_ge(hot, g * U + (j + 1))
                    eng.wait_ge(gathered[j], g * 16 + 16)
                    if heads or own is not None:
                        eng.wait_ge(owned, g * U + (j + 1))
                    eng.matmul(psum(j), m.onehot[:, j, 0:BN], m.rows[:, j, 0:width], start=True, stop=True).then_inc(used, 1)

        @block.vector
        def _(eng):
            def make(g, j, tile):
                if weight is None:
                    ins = eng.tensor_scalar(m.onehot[:, j, 0:BN], m.lane_of[:, 0:BN], near_lane[:, bass.ds(tile, 1)], None,
                                            ALU.is_equal)
                else:
                    ins = eng.tensor_scalar(m.onehot[:, j, 0:BN], m.lane_of[:, 0:BN], near_lane[:, bass.ds(tile, 1)],
                                            weight[:, bass.ds(tile, 1)], ALU.is_equal, ALU.mult)
                if heads:
                    eng.wait_ge(gathered[j], g * 16 + 16)
                    rows = m.rows[:, j, 0:D].rearrange("p (h d) -> p h d", h=HEADS)
                    ins = eng.tensor_tensor(rows, rows, bcast(m.S[:, bass.ds(tile, 1), :].rearrange("p a h -> p (a h)"), 2, HD), ALU.mult)
                ins.then_inc(hot, 1)

            def add(g, j, b):
                eng.wait_ge(used, g * U + (U + j + 1))
                to = m.sums[:, bass.ds(b, 1), 0:width].rearrange("p a d -> p (a d)")
                eng.wait_ge(added, g * U + (j + 1))
                eng.tensor_tensor(to, to, psum(j), ALU.add).then_inc(added, 1)

            eng.memset(m.sums[:, :, :], 0.0).then_inc(added, 1)
            if not heads:
                eng.memset(m.rows[:, :, D:D + 1], 1.0)
            for j in range(U):
                make(0, j, j)
            with eng.Fori(0, GROUPS - 1) as g:
                blocks = tile_blocks(nc, eng, tile_block, g * U)
                for j in range(U):
                    add(g, j, blocks[j])
                    make(g + 1, j, g * U + (U + j))
            blocks = tile_blocks(nc, eng, tile_block, TILES - U)
            for j in range(U):
                add(GROUPS - 1, j, blocks[j])
            eng.wait_ge(added, TILES + 1)


def node_step(nc, build):
    with Phase(nc) as ctx:
        step = ctx.sem("step")
        block = ctx.block()

        @block.vector
        def _(eng):
            c = Count()

            def do(ins):
                ins.then_inc(step, 1)
                eng.wait_ge(step, c.up())

            build(eng, do)


def batch_norm(nc, m, A, out):
    with Phase(nc) as ctx:
        sem = ctx.sem
        loaded, step, agg_ready, centred, squared, summed = sem("loaded"), sem("step"), sem("agg_ready"), sem("centred"), sem("squared"), sem("summed")
        var_ready, root_ready, done, stored = sem("var_ready"), sem("root_ready"), sem("done"), sem("stored")
        block = ctx.block()
        sums = m.sums[:, :, 0:D]
        mean = m.work[0:BN, 0, :]
        var = m.work[0:BN, 1, :]
        bias, gamma, beta = [m.bias[:, k * D:(k + 1) * D] for k in range(3)]

        @block.sync
        def _(eng):
            for to, name in ((bias, "L3_gnn_bias"), (gamma, "L3_gnn_bn_gamma"), (beta, "L3_gnn_bn_beta")):
                eng.dma_start(to, A[name].partition_broadcast(BN)).then_inc(loaded, 16)
            eng.wait_ge(done, 1)
            eng.dma_start(out.rearrange("(b p) d -> p b d", p=BN), m.x[:, :, :]).then_inc(stored, 16)
            eng.wait_ge(stored, 16)

        @block.tensor
        def _(eng):
            eng.wait_ge(agg_ready, 1)
            for b in range(NB):
                mm = eng.matmul(m.bank[0][0:BN, 0:D], m.ones[0:BN, 0:BN], m.nodes[:, b, :], start=(b == 0), stop=(b == NB - 1))
            mm.then_inc(summed, 1)
            eng.wait_ge(squared, 1)
            for b in range(NB):
                mm = eng.matmul(m.bank[1][0:BN, 0:D], m.ones[0:BN, 0:BN], sums[:, b, :], start=(b == 0), stop=(b == NB - 1))
            mm.then_inc(summed, 1)

        @block.scalar
        def _(eng):
            eng.wait_ge(centred, 1)
            eng.activation(sums, m.nodes[:, :, :], ACT.Square).then_inc(squared, 1)
            eng.wait_ge(var_ready, 1)
            eng.activation(var, var, ACT.Sqrt).then_inc(root_ready, 1)

        @block.vector
        def _(eng):
            c = Count()

            def do(ins):
                ins.then_inc(step, 1)
                eng.wait_ge(step, c.up())

            do(eng.tensor_tensor(m.nodes, m.nodes, sums, ALU.add))
            do(eng.tensor_tensor(m.nodes, m.nodes, bcast(m.dinv[:, :], 2, D), ALU.mult))
            eng.wait_ge(loaded, 48)
            eng.tensor_tensor(m.nodes, m.nodes, bcast(bias, 1, NB), ALU.add).then_inc(agg_ready, 1)
            eng.wait_ge(summed, 1)
            do(eng.tensor_scalar(mean, m.bank[0][0:BN, 0:D], 1.0 / N, None, ALU.mult))
            eng.tensor_tensor(m.nodes, m.nodes, bcast(mean, 1, NB), ALU.subtract).then_inc(centred, 1)
            eng.wait_ge(summed, 2)
            eng.tensor_scalar(var, m.bank[1][0:BN, 0:D], 1.0 / N, EPS, ALU.mult, ALU.add).then_inc(var_ready, 1)
            eng.wait_ge(root_ready, 1)
            do(eng.reciprocal(var, var))
            do(eng.tensor_tensor(var, var, gamma, ALU.mult))
            do(eng.tensor_tensor(m.nodes, m.nodes, bcast(var, 1, NB), ALU.mult))
            do(eng.tensor_tensor(m.nodes, m.nodes, bcast(beta, 1, NB), ALU.add))
            eng.scalar_tensor_tensor(out=flat(m.x[:, :, :]), in0=flat(m.nodes), scalar=0.0, in1=flat(m.x[:, :, :]),
                                     op0=ALU.max, op1=ALU.add).then_inc(done, 1)


def flat(ap):
    return ap.rearrange("p b d -> p (b d)")


def turn_weights(nc, m, A):
    with Phase(nc) as ctx:
        loaded, turned, copied = [ctx.sem(n) for n in ("loaded", "turned", "copied")]
        block = ctx.block()
        raw = m.work[:, 0:2, :]

        @block.sync
        def _(eng):
            eng.dma_start(raw, A["L1_gnn_W_layer"].rearrange("(o p) i -> p o i", p=P)).then_inc(loaded, 16)

        @block.tensor
        def _(eng):
            eng.wait_ge(loaded, 16)
            for o in range(2):
                for i in range(2):
                    eng.transpose(m.bank[2 * o + i][:, 0:P], raw[:, o, i * P:(i + 1) * P], m.ident[:, :]).then_inc(turned, 1)

        @block.scalar
        def _(eng):
            for o in range(2):
                for i in range(2):
                    eng.wait_ge(turned, 2 * o + i + 1)
                    eng.activation(m.weights[:, i, o * P:(o + 1) * P], m.bank[2 * o + i][:, 0:P], ACT.Copy).then_inc(copied, 1)
            eng.wait_ge(copied, 4)


def gnn_kernel(nc, A, out, upto=99, dump=None):
    def scratch(name, rows, cols):
        return nc.dram_tensor(name, (rows, cols), F32, kind="Internal").ap()

    keys, values, feats, far2 = scratch("keys", N, D), scratch("values", N, D), scratch("feats", N, D), scratch("a2_rows", N, 1)
    typed, shared = scratch("typed", RELS * N, D), scratch("shared", N, D)
    records = scratch("records", P * (TILES + 1), 4)

    def by_k(w):
        return w.rearrange("(k p) n -> p k n", p=P)

    with ExitStack() as ctx:
        m = Memory(nc, ctx)
        col = [m.cols[:, k, :] for k in range(14)]
        load_inputs(nc, m, A)
        split_keys(nc, m)
        rank(nc, m, col[DST_BLOCK], NB + 1, col[DST_AT_LANE], col[DST_AT_TILE], m.starts[:, 1, :])
        target_order(nc, m, records)
        packs = [col[k][:, 0:COLS] for k in (PACK0, PACK1, PACK2)]
        rank(nc, m, col[SRC_LANE], BN, col[RAW_DST], col[RAW_TYPE])
        permute(nc, m, packs, col[RAW_DST], col[RAW_TYPE], COLS, packs)
        between_passes(nc, m)
        rank(nc, m, col[SRC_BLOCK], NB + 1, col[RAW_DST], col[RAW_TYPE], m.starts[:, 0, :])
        got = [m.edge[:, 0, k * TILES:(k + 1) * TILES] for k in range(3)]
        permute(nc, m, packs, col[RAW_DST], col[RAW_TYPE], TILES, got)
        source_order(nc, m, got)

        def qkv(eng, j, b, g, psum):
            if g == 0:
                return eng.tensor_tensor(m.nodes[:, bass.ds(b, 1), :].rearrange("p a d -> p (a d)"), psum, m.bias[:, 0:D], ALU.add)
            return eng.tensor_tensor(m.stage[:, j, 0:2 * D], psum, m.bias[:, D:3 * D], ALU.add)

        def blocks_of(table):
            return table.rearrange("(b p) d -> p b d", p=BN)

        def store_kv(b, j):
            for k, table in enumerate((keys, values)):
                yield (blocks_of(table)[:, bass.ds(b, 1), :].rearrange("p a d -> p (a d)"), m.stage[:, j, k * D:(k + 1) * D])

        loads = []
        for k, n in enumerate("qkv"):
            loads.append((m.weights[:, :, k * D:(k + 1) * D], by_k(A["L0_gnn_W" + n])))
            loads.append((m.bias[:, k * D:(k + 1) * D], A["L0_gnn_b" + n].partition_broadcast(BN)))
        project(nc, m, [(0, D), (D, 3 * D)], qkv, loads, store=store_kv, stored=2)
        edge_scores(nc, m, m.src_far, keys, D, additive=False)
        if upto == 1:
            return dump(m)
        softmax_weights(nc, m, HEADS, m.S, m.M, SCALE)
        if upto == 2:
            return dump(m)
        sum_over_edges(nc, m, m.src_lane, None, m.src_block, m.src_far, values, D + HEADS, heads=True)
        loads = [(m.weights[:, :, 0:D], by_k(A["L0_gnn_Wo"])), (m.bias[:, 0:D], A["L0_gnn_bo"].partition_broadcast(BN))]

        def add_to_x(eng, j, b, g, psum):
            to = m.x[:, bass.ds(b, 1), :].rearrange("p a d -> p (a d)")
            return eng.tensor_tensor(to, to, psum, ALU.add)

        project(nc, m, [(0, D)], add_to_x, loads, divide=True)
        node_step(nc, lambda eng, do: do(eng.tensor_tensor(m.x[:, :, :], m.x[:, :, :], bcast(m.bias[:, 0:D], 1, NB), ALU.add)))
        if upto == 3:
            return dump(m)

        turn_weights(nc, m, A)

        def feature(eng, j, b, g, psum):
            return eng.tensor_tensor(m.stage[:, j, 0:D], psum, m.bias[:, 0:D], ALU.add)

        def node_scores(eng, j, b):
            for k, a in enumerate((m.a1, m.a2)):
                ins = eng.scalar_tensor_tensor(out=m.stage[:, j, (k + 1) * D:(k + 2) * D], in0=m.stage[:, j, 0:D], scalar=1.0, in1=m.wa[:, k, :],
                                         op0=ALU.mult, op1=ALU.mult, accum_out=a[:, bass.ds(b, 1)])
            return ins

        loads = [(m.bias[:, 0:D], A["L1_gnn_b_layer"].partition_broadcast(BN)),
                 (m.wa[:, 0, :], A["L1_gnn_w_a1"].rearrange("a d -> (a d)").partition_broadcast(BN)),
                 (m.wa[:, 1, :], A["L1_gnn_w_a2"].rearrange("a d -> (a d)").partition_broadcast(BN)),
                 (m.ba[:, 0:1], A["L1_gnn_b_a1"].partition_broadcast(BN)),
                 (m.ba[:, 1:2], A["L1_gnn_b_a2"].partition_broadcast(BN))]
        project(nc, m, [(0, D)], feature, loads,
                store=lambda b, j: [(blocks_of(feats)[:, bass.ds(b, 1), :].rearrange("p a d -> p (a d)"), m.stage[:, j, 0:D])],
                stored=1, after=node_scores)

        def add_biases(eng, do):
            do(eng.tensor_scalar(m.a1[:, :], m.a1[:, :], m.ba[:, 0:1], None, ALU.add))
            do(eng.tensor_scalar(m.a2[:, :], m.a2[:, :], m.ba[:, 1:2], None, ALU.add))

        node_step(nc, add_biases)
        with Phase(nc) as inner:
            stored = inner.sem("a2_stored")
            block = inner.block()

            @block.sync
            def _(eng):
                with nc.allow_non_contiguous_dma("one value per node"):
                    eng.dma_start(far2.rearrange("(b p) o -> p (b o)", p=BN), m.a2[:, :]).then_inc(stored, 16)
                eng.wait_ge(stored, 16)

        edge_scores(nc, m, m.src_far, far2, 1, additive=True)
        softmax_weights(nc, m, 1, m.S1.unsqueeze(2), m.M1.unsqueeze(2), 1.0)
        sum_over_edges(nc, m, m.src_lane, m.S1, m.src_block, m.src_far, feats, D + 1)

        def divided(eng, do):
            do(eng.tensor_scalar(m.rstd[:, :], m.sums[:, :, D], 0.5, None, ALU.max))
            do(eng.reciprocal(m.rstd[:, :], m.rstd[:, :]))
            do(eng.tensor_tensor(m.nodes, m.sums[:, :, 0:D], bcast(m.rstd[:, :], 2, D), ALU.mult))
            do(eng.tensor_tensor(flat(m.x[:, :, :]), flat(m.x[:, :, :]), flat(m.nodes), ALU.add))

        node_step(nc, divided)
        if upto == 4:
            return dump(m)

        def relations(eng, j, b, g, psum):
            if g == 0:
                return eng.tensor_tensor(m.nodes[:, bass.ds(b, 1), :].rearrange("p a d -> p (a d)"), psum, m.bias[:, 0:D], ALU.add)
            return eng.tensor_copy(m.stage[:, j, (g - 1) * 2 * D:g * 2 * D], psum)

        loads = [(m.weights[:, :, 0:D], by_k(A["L2_gnn_self_W"])), (m.bias[:, 0:D], A["L2_gnn_self_b"].partition_broadcast(BN))]
        for r in range(RELS):
            loads.append((m.weights[:, :, (r + 1) * D:(r + 2) * D], by_k(A["L2_gnn_rel_W"][r, :, :])))
        by_relation = typed.rearrange("(r b p) d -> p r b d", r=RELS, p=BN)
        project(nc, m, [(0, D), (D, 3 * D), (3 * D, 5 * D)], relations, loads,
                store=lambda b, j: [(by_relation[:, :, bass.ds(b, 1), :].rearrange("p r a d -> p r (a d)"),
                                     m.stage[:, j, 0:RELS * D].rearrange("p (r d) -> p r d", r=RELS))],
                stored=1)
        sum_over_edges(nc, m, m.dst_lane, None, m.dst_block, m.dst_far[:, 0, :], typed, D + 2, own=m.dst_w)

        def mean_of_edges(eng, do):
            do(eng.tensor_scalar(m.rstd[:, :], m.sums[:, :, D], 1.0, None, ALU.max))
            do(eng.reciprocal(m.rstd[:, :], m.rstd[:, :]))
            do(eng.tensor_tensor(m.sums[:, :, 0:D], m.sums[:, :, 0:D], bcast(m.rstd[:, :], 2, D), ALU.mult))
            do(eng.tensor_tensor(m.nodes, m.nodes, m.sums[:, :, 0:D], ALU.add))
            do(eng.scalar_tensor_tensor(out=flat(m.x[:, :, :]), in0=flat(m.nodes), scalar=0.0, in1=flat(m.x[:, :, :]),
                                        op0=ALU.max, op1=ALU.add))
            do(eng.tensor_scalar(m.a1[:, :], m.sums[:, :, D + 1], 1.0, None, ALU.add))
            do(eng.tensor_scalar(m.a2[:, :], m.a1[:, :], 0.0, None, ALU.is_gt))
            do(eng.tensor_scalar(m.a1[:, :], m.a1[:, :], 1e-30, None, ALU.max))

        node_step(nc, mean_of_edges)
        with Phase(nc) as inner:
            rooted = inner.sem("rooted")
            block = inner.block()

            @block.scalar
            def _(eng):
                eng.activation(m.dinv[:, :], m.a1[:, :], ACT.Sqrt).then_inc(rooted, 1)
                eng.wait_ge(rooted, 1)

        def inverse_root(eng, do):
            do(eng.reciprocal(m.dinv[:, :], m.dinv[:, :]))
            do(eng.tensor_tensor(m.dinv[:, :], m.dinv[:, :], m.a2[:, :], ALU.mult))

        node_step(nc, inverse_root)
        if upto == 5:
            return dump(m)

        def scaled(eng, j, b, g, psum):
            return eng.tensor_scalar(m.nodes[:, bass.ds(b, 1), :].rearrange("p a d -> p (a d)"), psum,
                                     m.dinv[:, bass.ds(b, 1)], None, ALU.mult)

        project(nc, m, [(0, D)], scaled, [(m.weights[:, :, 0:D], by_k(A["L3_gnn_weight"]))],
                store=lambda b, j: [(blocks_of(shared)[:, bass.ds(b, 1), :], m.nodes[:, bass.ds(b, 1), :])], stored=1)
        sum_over_edges(nc, m, m.dst_lane, m.dst_w, m.dst_block, m.dst_far[:, 1, :], shared, D)
        batch_norm(nc, m, A, out)


_INS = ["x", "src", "dst", "edge_type_4", "edge_weight", "L0_gnn_Wq", "L0_gnn_bq", "L0_gnn_Wk", "L0_gnn_bk", "L0_gnn_Wv",
        "L0_gnn_bv", "L0_gnn_Wo", "L0_gnn_bo", "L1_gnn_W_layer", "L1_gnn_b_layer", "L1_gnn_w_a1", "L1_gnn_b_a1",
        "L1_gnn_w_a2", "L1_gnn_b_a2", "L2_gnn_self_W", "L2_gnn_self_b", "L2_gnn_rel_W", "L3_gnn_weight", "L3_gnn_bias",
        "L3_gnn_bn_gamma", "L3_gnn_bn_beta"]


def kernel(**inputs):
    import numpy as np
    import concourse.bacc as bacc
    from concourse.bass_utils import run_bass_kernel_spmd

    nc = bacc.Bacc("TRN2", target_bir_lowering=False, num_devices=1)
    arrays, A = {}, {}
    for name in _INS:
        a = np.ascontiguousarray(inputs[name])
        arrays["in_" + name] = a
        A[name] = nc.dram_tensor("in_" + name, a.shape, mybir.dt.from_np(a.dtype), kind="ExternalInput").ap()
    out = nc.dram_tensor("out", (N, D), F32, kind="ExternalOutput").ap()
    gnn_kernel(nc, A, out)
    return run_bass_kernel_spmd(nc, [arrays], core_ids=[0]).results[0]["out"]
```

```python
from contextlib import ExitStack

import concourse.bass as bass
from concourse import mybir

F32 = mybir.dt.float32
BF16 = mybir.dt.bfloat16
F16 = mybir.dt.float16
I32 = mybir.dt.int32
U32 = mybir.dt.uint32
U16 = mybir.dt.uint16
ALU = mybir.AluOpType
ACT = mybir.ActivationFunctionType
AX = mybir.AxisListType

P = 128
N, D, E = 3125, 256, 53125
BN = 125
NB = N // BN
HEADS, HD = 8, 32
RELS = 4
COLS = -(-E // P)
PADS = P * COLS - E
CHAINS = 4
CLEN = COLS // CHAINS
TILES = E // P + NB
U = 8
GROUPS = TILES // U
CH = 8
CT = TILES // CH
CU = CT * P
BU = 5
PU = 40
ROW = 264
BIG = 1.0e30
ROUND = 12582912.0
EPS = 1e-5
SCALE = HD ** -0.5
assert TILES % U == 0 and TILES % CH == 0 and TILES % PU == 0 and COLS % CHAINS == 0 and CLEN % 4 == 0
assert TILES * P >= E + NB * (P - 1)


class Count:

    def __init__(self):
        self.n = 0

    def up(self):
        self.n += 1
        return self.n


class Phase(ExitStack):

    number = 0

    def __init__(self, nc):
        super().__init__()
        self.nc, self.sems = nc, []
        Phase.number += 1
        self.number = Phase.number

    def __enter__(self):
        super().__enter__()
        self.callback(self.clear)
        return self

    def clear(self):
        self.nc.clear_and_free_semaphores(self.sems)
        self.nc.all_engine_barrier()

    def sem(self, name):
        self.sems.append(self.nc.alloc_semaphore(f"{name}_{self.number}"))
        return self.sems[-1]

    def block(self):
        return self.enter_context(self.nc.Block())


def bcast(ap, axis, n):
    ap = ap.unsqueeze(axis)
    shape = list(ap.shape)
    shape[axis] = n
    return ap.broadcast_to(shape)


def tile_blocks(nc, eng, table, first):
    return nc.values_load_multi_w_load_instructions(
        table[0:1, bass.ds(first, U)], engines=[eng.engine], min_val=0, max_val=NB - 1)[1]


class Memory:

    def __init__(self, nc, ctx):
        self.nc, self.ctx = nc, ctx
        sb, ps = self.sb, self.ps
        self.x = sb("x_nodes", [BN, NB, D], F32)
        self.acc = sb("acc", [P, CU + 1], F32)
        self.node = sb("node", [P, CU + 1], F32)
        self.edge = sb("edge", [P, 2, TILES * HEADS], F32)
        self.weights = sb("weights", [P, 2, 1280], F32)
        self.bias = sb("bias", [BN, 1280], F32)
        self.rows = sb("rows", [P, U, ROW], F32)
        self.work = sb("work", [P, U, D], F32)
        self.onehot = sb("onehot", [P, U, P], F32)
        self.turned = sb("turned", [P, U, P], F32)
        self.cols = sb("cols", [P, 14, COLS + 4], F32)
        self.src_lane = sb("src_lane", [P, TILES + U], F32)
        self.src_key = sb("src_key", [P, TILES], F32)
        self.src_far = sb("src_far", [P, TILES], I32)
        self.src_block = sb("src_block", [P, TILES], I32)
        self.sort = sb("sort", [P, 1760], F32)
        self.dst_lane = sb("dst_lane", [P, TILES + U], F32)
        self.dst_w = sb("dst_w", [P, TILES + U], F32)
        self.dst_far = sb("dst_far", [P, 2, TILES], I32)
        self.dst_block = sb("dst_block", [P, TILES], I32)
        self.index = sb("index", [P, PU], I32)
        self.ident = sb("ident", [P, P], F32)
        self.lane_of = sb("lane_of", [P, TILES], F32)
        self.lane_h = sb("lane_h", [P, TILES], F16)
        self.lane_id = sb("lane_id", [P, 2], F32)
        self.parts = sb("parts", [BN, 2, 3 * NB], BF16)
        self.ones = sb("ones", [P, P], F32)
        self.before = sb("before", [P, P], BF16)
        self.behind = sb("behind", [P, P], BF16)
        self.zeros_b = sb("zeros_b", [P, 512], BF16)
        self.zeros_wide = sb("zeros_wide", [P, COLS + 1], F32)
        self.stat = sb("stat", [BN, NB, 6], F32)
        self.mv = sb("mv", [BN, NB, 2], F32)
        self.rstd = sb("rstd", [BN, NB], F32)
        self.nbias = sb("nbias", [BN, NB], F32)
        self.a1 = sb("a1", [BN, NB], F32)
        self.a2 = sb("a2", [BN, NB], F32)
        self.dinv = sb("dinv", [BN, NB], F32)
        self.rden = sb("rden", [BN, NB, HEADS], F32)
        self.wa = sb("wa", [BN, 2, D], F32)
        self.ba = sb("ba", [BN, 2], F32)
        self.starts = sb("starts", [P, 2, 32], F32)
        self.small = sb("small", [P, 5, P], F32)
        self.bank = [ps(f"bank{i}", [P, 512], F32) for i in range(8)]
        self.ends = self.work[:, :, :].rearrange("p a b -> p (a b)")[:, 0:4 * TILES].rearrange("p (k t) -> p k t", k=4)
        self.lines = self.onehot[:, :, :].rearrange("p a b -> p (a b)").bitcast(F16).rearrange("p (s k e) -> p s k e", s=2, k=2)
        self.hots = self.turned[:, :, :].rearrange("p a b -> p (a b)").bitcast(BF16).rearrange("p (s k e) -> p s k e", s=2, k=2)
        self.q = [self.acc[0:BN, 0:NB * D // 2].bitcast(BF16), self.acc[0:BN, NB * D // 2:NB * D].bitcast(BF16),
                  self.edge[0:BN, 1, 0:NB * D // 2].bitcast(BF16)]
        self.dst_rec = self.node[:, 0:4 * TILES].rearrange("p (t c) -> p t c", c=4)
        self.sums = self.acc[0:BN, 0:NB * ROW].rearrange("p (b d) -> p b d", b=NB)
        self.nodes = self.node[0:BN, 0:NB * D].rearrange("p (b d) -> p b d", b=NB)
        self.S = self.edge[:, 0, :].rearrange("p (t h) -> p t h", h=HEADS)
        self.S1 = self.edge[:, 0, 0:TILES]
        self.M1 = self.edge[:, 1, 0:TILES]
        self.M = self.edge[:, 1, :].rearrange("p (t h) -> p t h", h=HEADS)
        self.stage = self.edge[:, :, :].rearrange("p a n -> p (a n)")[0:BN, 0:BU * 1280]\
            .rearrange("p (j c) -> p j c", j=BU)

    def sb(self, name, shape, dt):
        return self.ctx.enter_context(self.nc.sbuf_tensor(name, shape, dt))

    def ps(self, name, shape, dt):
        return self.ctx.enter_context(self.nc.psum_tensor(name, shape, dt))


def load_inputs(nc, m, A):
    with Phase(nc) as ctx:
        loaded = ctx.sem("loaded")
        padded = ctx.sem("padded")
        made = ctx.sem("made")
        step = ctx.sem("step")
        block = ctx.block()
        raw = m.cols[:, 8:12, 0:COLS].bitcast(I32)
        full = P - 1
        rest = E - full * COLS

        @block.sync
        def _(eng):
            eng.dma_start(m.x[:, :, :], A["x"].rearrange("(b p) d -> p b d", p=BN)).then_inc(loaded, 16)
            eng.wait_ge(padded, 2)
            for k, name in enumerate(("src", "dst", "edge_type_4", "edge_weight")):
                to = raw[:, k, :] if k < 3 else m.cols[:, 11, 0:COLS]
                eng.dma_start(to[0:full, :], A[name][0:full * COLS].rearrange("(p t) -> p t", p=full)).then_inc(loaded, 16)
                eng.dma_start(to[full:P, 0:rest], A[name][full * COLS:E].rearrange("(p t) -> p t", p=1)).then_inc(loaded, 16)
            eng.wait_ge(loaded, 16 * 9)

        @block.gpsimd
        def _(eng):
            c = Count()
            eng.memset(m.ident[:, :], 0.0).then_inc(made, 1)
            eng.memset(m.ones[:, :], 1.0).then_inc(made, 1)
            eng.memset(m.before[:, :], 0.0).then_inc(made, 1)
            eng.memset(m.zeros_b[:, :], 0.0).then_inc(made, 1)
            eng.memset(m.zeros_wide[:, :], 0.0).then_inc(made, 1)
            eng.iota(m.work[:, 0:2, :].rearrange("p a b -> p (a b)")[:, 0:TILES].bitcast(I32),
                     [[1, TILES]], base=0, channel_multiplier=0).then_inc(made, 1)
            eng.memset(m.behind[:, :], 0.0).then_inc(made, 1)
            eng.iota(m.work[:, 2, 0:1].bitcast(I32), [[1, 1]], base=0, channel_multiplier=1).then_inc(made, 1)
            eng.wait_ge(made, 8)
            eng.affine_select(out=m.ident[:, :], in_=m.ident[:, :], compare_op=ALU.not_equal, fill=1.0,
                              base=0, pattern=[[-1, P]], channel_multiplier=1).then_inc(made, 1)
            eng.affine_select(out=m.behind[:, :], in_=m.behind[:, :], compare_op=ALU.is_ge, fill=1.0,
                              base=-1, pattern=[[1, P]], channel_multiplier=-1).then_inc(made, 1)
            eng.affine_select(out=m.before[:, :], in_=m.before[:, :], compare_op=ALU.is_ge, fill=1.0,
                              base=0, pattern=[[-1, P]], channel_multiplier=1).then_inc(made, 1)
            eng.wait_ge(made, 11)

        @block.vector
        def _(eng):
            eng.memset(raw[:, 0:3, :], N).then_inc(padded, 1)
            eng.memset(m.cols[:, 11, :], 0.0).then_inc(padded, 1)
            eng.memset(m.cols[:, 0:8, :], 0.0).then_inc(step, 1)
            eng.memset(m.src_lane[:, :], -1.0).then_inc(step, 1)
            eng.memset(m.dst_lane[:, :], -1.0).then_inc(step, 1)
            eng.memset(m.dst_w[:, :], 0.0).then_inc(step, 1)
            eng.memset(m.rows[:, :, :], 1.0).then_inc(step, 1)
            eng.wait_ge(made, 8)
            iota = m.work[:, 0:2, :].rearrange("p a b -> p (a b)")[:, 0:TILES].bitcast(I32)
            eng.tensor_copy(m.lane_of[:, :], iota).then_inc(step, 1)
            eng.tensor_copy(m.lane_h[:, :], iota).then_inc(step, 1)
            eng.tensor_copy(m.lane_id[:, 0:1], m.work[:, 2, 0:1].bitcast(I32)).then_inc(step, 1)
            eng.wait_ge(step, 8)
            c = Count()
            c.n = 8
            floor_div(eng, step, c, m.lane_id[:, 1:2], m.lane_id[:, 0:1], NB)
            remainder(eng, step, c, m.lane_id[:, 1:2], m.lane_id[:, 0:1], m.lane_id[:, 1:2], NB)


def floor_div(eng, step, c, q, x, d):
    eng.tensor_scalar(q, x, 1.0 / d, 0.5 / d - 0.5, ALU.mult, ALU.add).then_inc(step, 1)
    eng.wait_ge(step, c.up())
    eng.tensor_scalar(q, q, ROUND, ROUND, ALU.add, ALU.subtract).then_inc(step, 1)
    eng.wait_ge(step, c.up())


def remainder(eng, step, c, r, x, q, d):
    eng.scalar_tensor_tensor(out=r, in0=q, scalar=-float(d), in1=x, op0=ALU.mult, op1=ALU.add).then_inc(step, 1)
    eng.wait_ge(step, c.up())


(SRC_LANE, SRC_BLOCK, DST_LANE, DST_BLOCK, SRC, DST, AT_LANE, AT_TILE, RAW_SRC, RAW_DST, RAW_TYPE, WEIGHT,
 DST_AT_LANE, DST_AT_TILE) = range(14)
MID = 1600
KEYS_LANE = 128
KEYS_BLOCK = 28
CB = 16
HALF = 8


class Rank:

    def __init__(self, m, name, ctx, key, keys, lane, tile, starts=None):
        def sem(what):
            return ctx.sem(f"{name}_{what}")

        self.m, self.key, self.keys, self.starts = m, key, keys, starts
        self.lane, self.tile = lane, tile
        self.step, self.hot, self.counted = sem("step"), sem("hot"), sem("counted")
        self.scanned, self.placed, self.noted = sem("scanned"), sem("placed"), sem("noted")
        self.key_h = m.sort[:, 0:COLS // 2].bitcast(F16)
        wide = COLS + 4
        self.oh = m.sort[:, COLS // 2:COLS // 2 + 2 * wide].bitcast(BF16).rearrange("p (u t) -> p u t", u=4)
        self.run = m.acc[:, 0:4 * wide].rearrange("p (u t) -> p u t", u=4)
        self.part = m.acc[:, 8 * COLS:10 * COLS].rearrange("p (u t) -> p u t", u=2)
        self.steps = [m.bank[u][:, 0:COLS + 1] for u in range(4)]

    def tensor(self, eng):
        m = self.m
        with eng.Fori(0, self.keys // 4) as i:
            for u in range(4):
                eng.wait_ge(self.hot, i * 4 + (u + 1))
                eng.matmul(self.steps[u], m.before[:, :], self.oh[:, u, 2:COLS + 3], start=True, stop=False)
                eng.matmul(self.steps[u], m.behind[:, :], self.oh[:, u, 1:COLS + 2], start=False, stop=True)\
                   .then_inc(self.counted, 1)

    def vector(self, eng):
        m, place, run = self.m, self.lane, self.run
        c = Count()

        def do(ins):
            ins.then_inc(self.step, 1)
            eng.wait_ge(self.step, c.up())

        do(eng.tensor_copy(self.key_h, self.key))
        do(eng.memset(run[:, 3, COLS:COLS + 1], 0.0))
        do(eng.memset(self.oh[:, :, :], 0.0))
        do(eng.memset(place, 0.0))

        def next_hot(k, u):
            eng.tensor_scalar(self.oh[:, u, 2:COLS + 2], self.key_h, m.lane_of[:, bass.ds(k, 1)], None, ALU.is_equal)\
               .then_inc(self.hot, 1)

        def pick(u):
            eng.copy_predicated(place, self.oh[:, u, 2:COLS + 2].bitcast(U16), run[:, u, 0:COLS]).then_inc(self.placed, 1)

        for u in range(4):
            next_hot(u, u)
        cum = m.small[:, 0, :]

        def four_keys(i, later):
            def scan(u):
                eng.wait_ge(self.counted, i * 4 + (u + 1))
                eng.tensor_tensor_scan(run[:, u, 0:COLS + 1], self.steps[u], m.zeros_wide[:, 0:COLS + 1],
                                       run[:, (u + 3) % 4, COLS:COLS + 1], ALU.add, ALU.add).then_inc(self.scanned, 1)

            def scanned(u):
                eng.wait_ge(self.scanned, i * 4 + (u + 1))

            def placed(u):
                eng.wait_ge(self.placed, i * 4 + (u + 1))

            if later and self.starts is not None:
                eng.wait_ge(self.noted, i)
            scan(0)
            if later:
                pick(3)
            scanned(0)
            scan(1)
            if later:
                placed(-1)
                next_hot(i * 4 + 3, 3)
            pick(0)
            scanned(1)
            scan(2)
            placed(0)
            next_hot(i * 4 + 4, 0)
            pick(1)
            scanned(2)
            scan(3)
            placed(1)
            next_hot(i * 4 + 5, 1)
            pick(2)
            scanned(3)
            if self.starts is not None:
                eng.tensor_copy(cum[:, bass.ds(i * 4, 4)], run[:, :, COLS]).then_inc(self.noted, 1)
            placed(2)
            next_hot(i * 4 + 6, 2)

        four_keys(0, False)
        with eng.Fori(1, self.keys // 4) as i:
            four_keys(i, True)
        pick(3)
        eng.wait_ge(self.placed, self.keys)
        if self.starts is not None:
            n = NB + 1
            total_k, tiles_k, rest, off = [m.small[:, k, 0:n] for k in (1, 2, 3, 4)]
            do(eng.tensor_copy(total_k, cum[:, 0:n]))
            do(eng.tensor_tensor(total_k[:, 1:n], cum[:, 1:n], cum[:, 0:n - 1], ALU.subtract))
            floor_div(eng, self.step, c, tiles_k, total_k, P)
            remainder(eng, self.step, c, rest, total_k, tiles_k, P)
            do(eng.tensor_scalar(rest, rest, 0.0, None, ALU.is_gt))
            do(eng.tensor_tensor(tiles_k, tiles_k, rest, ALU.add))
            do(eng.tensor_tensor_scan(rest, tiles_k, m.zeros_wide[:, 0:n], 0.0, ALU.add, ALU.add))
            do(eng.tensor_tensor(self.starts[:, 0:n], rest, tiles_k, ALU.subtract))
            do(eng.memset(self.starts[:, n - 1:n], float(TILES)))
            do(eng.scalar_tensor_tensor(out=off, in0=self.starts[:, 0:n], scalar=float(P), in1=cum[:, 0:n],
                                        op0=ALU.mult, op1=ALU.subtract))
            do(eng.tensor_tensor(off, off, total_k, ALU.add))
            for k in range(n):
                part = self.part[:, k % 2, :]
                do(eng.tensor_scalar(part, self.key_h, float(k), off[:, k:k + 1], ALU.is_equal, ALU.mult))
                do(eng.tensor_tensor(place, place, part, ALU.add))
        floor_div(eng, self.step, c, self.tile, place, P)
        remainder(eng, self.step, c, place, place, self.tile, P)


class Permute:

    def __init__(self, m, name, ctx, values, lane, tile, tiles, out):
        def sem(what):
            return ctx.sem(f"{name}_{what}")

        self.m, self.values, self.lane, self.tile, self.tiles, self.out = m, values, lane, tile, tiles, out
        self.ready, self.scaled, self.moved, self.step = sem("ready"), sem("scaled"), sem("moved"), sem("step")
        self.at_tile = m.sort[:, 0:2 * tiles].bitcast(F16).rearrange("p (u t) -> p u t", u=4)
        at = 2 * tiles
        self.at_lane = m.sort[:, at:at + 2 * P].bitcast(F16).rearrange("p (u q) -> p u q", u=4)
        self.valued = m.sort[:, at + 2 * P:at + 6 * P].bitcast(F16).rearrange("p (u v q) -> p u v q", u=4, v=2)
        self.bank = [m.bank[4 + v][:, 0:tiles] for v in range(2)]

    def tensor(self, eng):
        m = self.m
        eng.wait_ge(self.ready, 1)
        for v in range(2):
            eng.matmul(self.bank[v], m.behind[:, :], m.zeros_b[:, 0:self.tiles], start=True, stop=False,
                       skip_group_check=True)
        with eng.Fori(0, COLS // CB) as i:
            for u in range(CB):
                if u % 2:
                    eng.wait_ge(self.scaled, i * (CB // 2) + (u // 2 + 1))
                else:
                    eng.wait_ge(self.ready, i * CB + (u + 1))
                for v in range(2):
                    mm = eng.matmul(self.bank[v], self.valued[:, u % 4, v, :], self.at_tile[:, u % 4, :],
                                    start=False, stop=True, skip_group_check=True)
                mm.then_inc(self.moved, 1)

    def scalar(self, eng):
        eng.activation(self.m.small[:, 4, P - 1:P], self.m.zeros_b[:, 0:1], ACT.Copy)
        with eng.Fori(0, COLS // CB) as i:
            for u in range(1, CB, 2):
                eng.wait_ge(self.ready, i * CB + (u + 1))
                for v in range(2):
                    last = eng.activation(self.valued[:, u % 4, v, :], self.at_lane[:, u % 4, :], ACT.Copy,
                                          scale=self.values[v][:, bass.ds(i * CB + u, 1)])
                last.then_inc(self.scaled, 1)

    def vector(self, eng):
        m = self.m

        def one_hots(u, column):
            eng.tensor_scalar(self.at_tile[:, u, :], m.lane_h[:, 0:self.tiles], self.tile[:, bass.ds(column, 1)], None,
                              ALU.is_equal)
            if u % 2:
                eng.tensor_scalar(self.at_lane[:, u, :], m.lane_h[:, 0:P], self.lane[:, bass.ds(column, 1)], None,
                                  ALU.is_equal).then_inc(self.ready, 1)
            else:
                for v in range(2):
                    last = eng.tensor_scalar(self.valued[:, u, v, :], m.lane_h[:, 0:P], self.lane[:, bass.ds(column, 1)],
                                             self.values[v][:, bass.ds(column, 1)], ALU.is_equal, ALU.mult)
                last.then_inc(self.ready, 1)

        eng.drain()
        for u in range(CB):
            if u >= 4:
                eng.wait_ge(self.moved, u - 3)
            one_hots(u % 4, u)
        with eng.Fori(1, COLS // CB) as i:
            for u in range(CB):
                eng.wait_ge(self.moved, i * CB + (u - 3))
                one_hots(u % 4, i * CB + u)
        eng.wait_ge(self.moved, COLS)
        for v in range(2):
            eng.tensor_copy(self.out[v], self.bank[v]).then_inc(self.step, 1)
        eng.wait_ge(self.step, 2)


def sort_edges(nc, m, table):
    with Phase(nc) as ctx:
        sem = ctx.sem
        step, blank, recorded = sem("step"), sem("blank"), sem("recorded")
        filled, copied, issued, back = sem("filled"), sem("copied"), sem("issued"), sem("back")
        landed, told = [sem("landed0"), sem("landed1")], sem("told")
        block = ctx.block()
        col = [m.cols[:, k, 0:COLS] for k in range(14)]
        got = [m.edge[:, 0, k * TILES:(k + 1) * TILES] for k in range(2)]
        by_target = Rank(m, "by_target", ctx, col[DST_BLOCK], KEYS_BLOCK, col[DST_AT_LANE], col[DST_AT_TILE], m.starts[:, 1, :])
        by_lane = Rank(m, "by_lane", ctx, col[SRC_LANE], KEYS_LANE, col[AT_LANE], col[AT_TILE])
        to_lane = Permute(m, "to_lane", ctx, [col[SRC], col[DST]], col[AT_LANE], col[AT_TILE], COLS, [col[SRC], col[DST]])
        by_block = Rank(m, "by_block", ctx, col[SRC_BLOCK], KEYS_BLOCK, col[AT_LANE], col[AT_TILE], m.starts[:, 0, :])
        to_block = Permute(m, "to_block", ctx, [col[SRC], col[DST]], col[AT_LANE], col[AT_TILE], TILES, got)
        blanks = m.node[:, 0:4 * (TILES + 1)].rearrange("p (t c) -> p t c", c=4)
        place = m.node[:, 1764:1764 + COLS].bitcast(I32)
        record = m.node[:, 2600:2600 + 4 * COLS].rearrange("p (t c) -> p t c", c=4)
        staged_record = m.rows[:, 0, 0:8 * HALF].rearrange("p (s a c) -> p s a c", s=2, c=4)
        staged_place = m.index[:, 0:2 * HALF].rearrange("p (s a) -> p s a", s=2)

        @block.sync
        def _(eng):
            eng.wait_ge(blank, 1)
            eng.dma_start(table.rearrange("(p t) c -> p t c", p=P), blanks).then_inc(filled, 16)
            for s in range(2):
                eng.wait_ge(landed[s], 16 * COLS // 2)
            eng.dma_start(m.dst_rec[:, :, :], table.rearrange("(p t) c -> p t c", p=P)[:, 0:TILES, :]).then_inc(back, 16)

        @block.gpsimd
        def _(eng):
            eng.wait_ge(filled, 16)
            eng.wait_ge(recorded, 2)

            def halves(i, later):
                for s in range(2):
                    if later:
                        eng.wait_ge(landed[s], i * (16 * HALF))
                    at = i * (2 * HALF) + s * HALF
                    eng.tensor_copy(staged_record[:, s, :, :], record[:, bass.ds(at, HALF), :])
                    eng.tensor_copy(staged_place[:, s, :], place[:, bass.ds(at, HALF)]).then_inc(copied, 1)
                    eng.wait_ge(copied, i * 2 + (s + 1))
                    eng.sem_inc(issued, 1)
                    for j in range(HALF):
                        eng.indirect_dma_start(
                            out=table, out_offset=bass.IndirectOffsetOnAxis(ap=staged_place[:, s, j:j + 1].bitcast(U32), axis=0),
                            in_=staged_record[:, s, j, :], in_offset=None).then_inc(landed[s], 16)

            halves(0, False)
            with eng.Fori(1, COLS // (2 * HALF)) as i:
                halves(i, True)

            c = Count()

            def do(ins):
                ins.then_inc(told, 1)
                eng.wait_ge(told, c.up())

            count, begun = [m.edge[:, 1, k * TILES:(k + 1) * TILES] for k in range(2)]
            do(eng.memset(count, 0.0))
            for b in range(1, NB):
                do(eng.tensor_scalar(begun, m.lane_of[:, :], m.starts[:, 1, b:b + 1], None, ALU.is_ge))
                do(eng.tensor_tensor(count, count, begun, ALU.add))
            do(eng.tensor_copy(m.dst_block[:, :], count))
            eng.wait_ge(back, 16)
            do(eng.tensor_copy(m.dst_lane[:, 0:TILES], m.dst_rec[:, :, 0]))
            do(eng.tensor_copy(m.dst_far[:, 1, :], m.dst_rec[:, :, 1]))
            do(eng.tensor_copy(m.dst_far[:, 0, :], m.dst_rec[:, :, 2]))
            do(eng.tensor_copy(m.dst_w[:, 0:TILES], m.dst_rec[:, :, 3]))

        @block.tensor
        def _(eng):
            by_target.tensor(eng)
            by_lane.tensor(eng)
            to_lane.tensor(eng)
            by_block.tensor(eng)
            to_block.tensor(eng)

        @block.scalar
        def _(eng):
            to_lane.scalar(eng)
            to_block.scalar(eng)

        @block.vector
        def _(eng):
            c = Count()

            def do(ins):
                ins.then_inc(step, 1)
                eng.wait_ge(step, c.up())

            do(eng.memset(blanks, 0.0))
            eng.memset(blanks[:, :, 0:1], -1.0).then_inc(blank, 1)
            src, dst, typ = [m.acc[:, k * COLS:(k + 1) * COLS] for k in (10, 11, 12)]
            do(eng.tensor_copy(src, col[RAW_SRC].bitcast(I32)))
            do(eng.tensor_copy(dst, col[RAW_DST].bitcast(I32)))
            do(eng.tensor_copy(typ, col[RAW_TYPE].bitcast(I32)))
            floor_div(eng, step, c, col[SRC_BLOCK], src, BN)
            remainder(eng, step, c, col[SRC_LANE], src, col[SRC_BLOCK], BN)
            floor_div(eng, step, c, col[DST_BLOCK], dst, BN)
            remainder(eng, step, c, record[:, :, 0], dst, col[DST_BLOCK], BN)
            do(eng.tensor_copy(record[:, :, 1], src))
            do(eng.scalar_tensor_tensor(out=record[:, :, 2], in0=typ, scalar=float(N), in1=src, op0=ALU.mult, op1=ALU.add))
            eng.tensor_copy(record[:, :, 3], col[WEIGHT]).then_inc(recorded, 1)
            do(eng.tensor_scalar(col[SRC], src, -float(MID), None, ALU.add))
            do(eng.tensor_scalar(col[DST], dst, -float(MID), None, ALU.add))

            by_target.vector(eng)
            eng.scalar_tensor_tensor(out=place, in0=col[DST_AT_LANE], scalar=float(TILES + 1),
                                     in1=col[DST_AT_TILE], op0=ALU.mult, op1=ALU.add).then_inc(recorded, 1)
            by_lane.vector(eng)
            to_lane.vector(eng)
            do(eng.tensor_scalar(src, col[SRC], float(MID), None, ALU.add))
            floor_div(eng, step, c, col[SRC_BLOCK], src, BN)
            remainder(eng, step, c, col[SRC], src, col[SRC_BLOCK], BN)
            do(eng.tensor_scalar(col[SRC], col[SRC], 1.0, None, ALU.add))
            by_block.vector(eng)
            to_block.vector(eng)

            def kept(ap):
                return ap.rearrange("p (t c) -> p c t", c=CH)

            def of(ap):
                return ap.rearrange("p (c t) -> p c t", c=CH)

            block_of = m.edge[:, 0, 2 * TILES:3 * TILES]
            partial = [m.acc[:, k * TILES:(k + 1) * TILES] for k in range(2)]
            for k in range(2):
                do(eng.memset(partial[k], 0.0))
            for b in range(1, NB):
                if b > 2:
                    eng.wait_ge(step, c.n - 1)
                eng.scalar_tensor_tensor(out=partial[b % 2], in0=m.lane_of[:, :], scalar=m.starts[:, 0, b:b + 1],
                                         in1=partial[b % 2], op0=ALU.is_ge, op1=ALU.add).then_inc(step, 1)
                c.up()
            eng.wait_ge(step, c.n)
            do(eng.tensor_tensor(block_of, partial[0], partial[1], ALU.add))

            do(eng.tensor_scalar(kept(m.src_lane[:, 0:TILES]), of(got[0]), -1.0, None, ALU.add))
            do(eng.tensor_scalar(kept(m.src_far[:, :]), of(got[1]), float(MID), None, ALU.add))
            do(eng.tensor_copy(kept(m.src_block[:, :]), of(block_of)))
            do(eng.tensor_scalar(got[1], got[0], 0.0, float(BN + 1), ALU.is_equal, ALU.mult))
            do(eng.tensor_tensor(got[0], got[0], got[1], ALU.add))
            do(eng.scalar_tensor_tensor(out=got[0], in0=block_of, scalar=float(BN + 1), in1=got[0], op0=ALU.mult, op1=ALU.add))
            do(eng.tensor_scalar(kept(m.src_key[:, :]), of(got[0]), BIG, None, ALU.mult))
            do(eng.tensor_copy(m.ends[:, 0, :], m.src_lane[:, 0:TILES]))
            do(eng.tensor_copy(kept(m.ends[:, 2, :]), of(block_of)))
            do(eng.tensor_copy(block_of, m.src_far[:, :]))
            floor_div(eng, step, c, m.ends[:, 3, :], block_of, BN)
            remainder(eng, step, c, m.ends[:, 1, :], block_of, m.ends[:, 3, :], BN)


def lay_out_ends(nc, m, lines):
    with Phase(nc) as ctx:
        turned, copied, stored = [ctx.sem(n) for n in ("turned", "copied", "stored")]
        block = ctx.block()
        C = TILES // 4
        staged = m.rows[0:C, :, :].rearrange("p a b -> p (a b)")[:, 0:4 * 2 * P].bitcast(F16)\
            .rearrange("p (k c e) -> p k c e", k=4, c=4)

        @block.tensor
        def _(eng):
            for k in range(4):
                for c in range(4):
                    tr = eng.transpose(m.bank[k][0:C, c * P:(c + 1) * P], m.ends[:, k, c * C:(c + 1) * C], m.ident[:, :])
                tr.then_inc(turned, 1)

        @block.vector
        def _(eng):
            for k in range(4):
                eng.wait_ge(turned, k + 1)
                eng.tensor_copy(staged[:, k, :, :].rearrange("p c e -> p (c e)"), m.bank[k][0:C, :]).then_inc(copied, 1)

        @block.sync
        def _(eng):
            for k in range(4):
                eng.wait_ge(copied, k + 1)
                eng.dma_start(lines[k:k + 1, :].rearrange("k (c p e) -> p (k c) e", c=4, p=C), staged[:, k, :, :]).then_inc(stored, 16)
            eng.wait_ge(stored, 16 * 4)


def split_q(nc, m):
    with Phase(nc) as ctx:
        first, less, second, last = [ctx.sem(n) for n in ("first", "less", "second", "last")]
        block = ctx.block()
        W = BU * D
        part = [slice(i * W, (i + 1) * W) for i in range(NB // BU)]
        q = m.node[0:BN, 0:NB * D]

        @block.scalar
        def _(eng):
            for i, p in enumerate(part):
                eng.activation(m.q[0][:, p], q[:, p], ACT.Copy).then_inc(first, 1)
            for i, p in enumerate(part):
                eng.wait_ge(less, i + 1)
                eng.activation(m.q[1][:, p], q[:, p], ACT.Copy).then_inc(second, 1)

        @block.vector
        def _(eng):
            for i, p in enumerate(part):
                eng.wait_ge(first, i + 1)
                eng.tensor_tensor(q[:, p], q[:, p], m.q[0][:, p], ALU.subtract).then_inc(less, 1)
            for i, p in enumerate(part):
                eng.wait_ge(second, i + 1)
                eng.tensor_tensor(m.q[2][:, p], q[:, p], m.q[1][:, p], ALU.subtract).then_inc(last, 1)
            eng.wait_ge(last, len(part))


def norm_stats(eng, step, c, m):
    for b in range(NB):
        eng.bn_stats(m.stat[:, b, :], m.x[:, b, :]).then_inc(step, 1)
        c.up()
    eng.wait_ge(step, c.n)
    for b in range(NB):
        eng.bn_aggr(m.mv[:, b, :], m.stat[:, b, :]).then_inc(step, 1)
        c.up()
    eng.wait_ge(step, c.n)
    eng.tensor_scalar(m.rstd[:, :], m.mv[:, :, 1], EPS, None, ALU.add).then_inc(step, 1)
    eng.wait_ge(step, c.up())


def project(nc, m, groups, finish, loads, divide=False, store=None, stored=0, after=None):
    with Phase(nc) as ctx:
        sem = ctx.sem
        step, var_ready, root_ready, scale_ready = sem("step"), sem("var_ready"), sem("root_ready"), sem("scale_ready")
        loaded, h_ready, turned, copied = sem("loaded"), sem("h_ready"), sem("turned"), sem("copied")
        summed, taken, noted = sem("summed"), sem("taken"), sem("noted")
        out_done = [sem(f"out_done{j}") for j in range(BU)]
        block = ctx.block()
        G = len(groups)
        TURNS = NB // BU
        h = m.work[0:BN, 0:BU, :]
        hT = [t[:, :, :].rearrange("p a b -> p (a b)")[:, 0:BU * BN].rearrange("p (j n) -> p j n", j=BU)
              for t in (m.turned, m.onehot)]

        def turned_psum(j, k):
            return m.bank[j % 3][:, k * P:k * P + BN]

        def out_psum(j, g):
            a, z = groups[g]
            return m.bank[3 + (j * G + g) % BU][0:BN, 0:z - a]

        @block.sync
        def _(eng):
            for to, of in loads:
                eng.dma_start(to, of).then_inc(loaded, 16)
            if store is not None:
                with eng.Fori(0, TURNS) as i:
                    for j in range(BU):
                        eng.wait_ge(taken, i * (BU * G) + (BU + j * G + G))
                        for to, of in store(i * BU + j, j):
                            eng.dma_start(to, of).then_inc(out_done[j], 16)
                for j in range(BU):
                    eng.wait_ge(out_done[j], 16 * stored * TURNS)
            eng.wait_ge(loaded, 16 * len(loads))

        @block.scalar
        def _(eng):
            if not divide:
                eng.wait_ge(var_ready, 1)
                eng.activation(m.rstd[:, :], m.rstd[:, :], ACT.Sqrt).then_inc(root_ready, 1)
                eng.wait_ge(scale_ready, 1)
            with eng.Fori(0, TURNS) as i:
                if not divide:
                    for j in range(BU):
                        b = i * BU + j
                        eng.wait_ge(turned, i * BU + (j + 1))
                        eng.activation(h[:, j, :], m.x[:, bass.ds(b, 1), :].rearrange("p a d -> p (a d)"), ACT.Relu,
                                       bias=m.nbias[:, bass.ds(b, 1)], scale=m.rstd[:, bass.ds(b, 1)]).then_inc(h_ready, 1)
                for j in range(BU):
                    eng.wait_ge(turned, i * BU + (BU + j + 1))
                    for k in range(2):
                        cp = eng.activation(hT[k][:, j, :], turned_psum(j, k), ACT.Copy)
                    cp.then_inc(copied, 1)

        @block.tensor
        def _(eng):
            eng.sem_inc(turned, BU)
            eng.wait_ge(loaded, 16 * len(loads))
            with eng.Fori(0, TURNS) as i:
                for j in range(BU):
                    eng.wait_ge(h_ready, i * BU + (j + 1))
                    if j >= 3:
                        eng.wait_ge(copied, i * BU + (j - 2))
                    for k in range(2):
                        tr = eng.transpose(turned_psum(j, k), h[:, j, k * P:(k + 1) * P], m.ident[0:BN, 0:BN])
                    tr.then_inc(turned, 1)
                for j in range(BU):
                    eng.wait_ge(copied, i * BU + (j + 1))
                    for g, (a, z) in enumerate(groups):
                        eng.wait_ge(taken, i * (BU * G) + (j * G + g + 1))
                        for k in range(2):
                            mm = eng.matmul(out_psum(j, g), hT[k][:, j, :], m.weights[:, k, a:z],
                                            start=(k == 0), stop=(k == 1))
                        mm.then_inc(summed, 1)

        @block.vector
        def _(eng):
            c = Count()
            eng.sem_inc(taken, BU)
            if divide:
                eng.tensor_scalar(m.rden[:, :, :], m.sums[:, :, D:D + HEADS], 0.5, None, ALU.max).then_inc(step, 1)
                eng.wait_ge(step, c.up())
                eng.reciprocal(m.rden[:, :, :], m.rden[:, :, :]).then_inc(step, 1)
                eng.wait_ge(step, c.up())
            else:
                norm_stats(eng, step, c, m)
                eng.sem_inc(var_ready, 1)
                eng.wait_ge(root_ready, 1)
                eng.reciprocal(m.rstd[:, :], m.rstd[:, :]).then_inc(step, 1)
                eng.wait_ge(step, c.up())
                eng.scalar_tensor_tensor(out=m.nbias[:, :], in0=m.mv[:, :, 0], scalar=-1.0, in1=m.rstd[:, :],
                                         op0=ALU.mult, op1=ALU.mult).then_inc(scale_ready, 1)
            eng.wait_ge(loaded, 16 * len(loads))
            def turn_of_blocks(i, later):
                if divide:
                    for j in range(BU):
                        b = i * BU + j
                        eng.wait_ge(turned, i * BU + (j + 1))
                        eng.tensor_tensor(h[:, j, :].rearrange("p (h d) -> p h d", h=HEADS),
                                          m.sums[:, bass.ds(b, 1), 0:D].rearrange("p a (h d) -> p (a h) d", h=HEADS),
                                          bcast(m.rden[:, bass.ds(b, 1), :].rearrange("p a h -> p (a h)"), 2, HD),
                                          ALU.mult).then_inc(h_ready, 1)
                if after is not None and later:
                    eng.wait_ge(noted, i * BU)
                for j in range(BU):
                    b = i * BU + j
                    if store is not None and later:
                        eng.wait_ge(out_done[j], i * (16 * stored))
                    for g in range(G):
                        eng.wait_ge(summed, i * (BU * G) + (j * G + g + 1))
                        finish(eng, j, b, g, out_psum(j, g)).then_inc(taken, 1)
                if after is not None:
                    for j in range(BU):
                        eng.wait_ge(taken, i * (BU * G) + (BU + j * G + G))
                        after(eng, j, i * BU + j).then_inc(noted, 1)

            turn_of_blocks(0, False)
            with eng.Fori(1, TURNS) as i:
                turn_of_blocks(i, True)


def gather_tiles(eng, nc, m, sems, index, table, width, used, copied, issued):
    with eng.Fori(0, TILES // PU) as q:
        for u in range(PU):
            if u % (PU // 2) == 0:
                eng.tensor_copy(m.index[:, u:u + PU // 2], index[:, bass.ds(q * PU + u, PU // 2)]).then_inc(copied, 1)
                eng.wait_ge(copied, q * 2 + (u * 2 // PU + 1))
            eng.wait_ge(used, q * PU + (u + 1))
            eng.sem_inc(issued, 1)
            eng.indirect_dma_start(out=m.rows[:, u % U, 0:width], out_offset=None, in_=table,
                                   in_offset=bass.IndirectOffsetOnAxis(ap=m.index[:, u:u + 1].bitcast(U32), axis=0))\
               .then_inc(sems[u % U], 16)


def edge_scores(nc, m, table, lines):
    HU = U // 2
    with Phase(nc) as ctx:
        sem = ctx.sem
        gathered = [sem(f"gathered{j}") for j in range(U)]
        laid = [sem("laid0"), sem("laid1")]
        used, copied, issued = sem("used"), sem("copied"), sem("issued")
        hot, near, mixed = sem("hot"), sem("near"), sem("mixed")
        block = ctx.block()
        lines_in = [m.lines[0:BN, h, 0, :] for h in range(2)]
        onehot = [m.hots[0:BN, h, 0, :] for h in range(2)]

        @block.gpsimd
        def _(eng):
            gather_tiles(eng, nc, m, gathered, m.src_far, table, D, used, copied, issued)

        @block.sync
        def _(eng):
            def halves(g, later):
                for h in range(2):
                    if later:
                        eng.wait_ge(hot, g * 2 + (h - 1))
                    eng.dma_start(lines_in[h], lines[0, bass.ds((g * 2 + h) * (HU * P), HU * P)].partition_broadcast(BN))\
                       .then_inc(laid[h], 16)

            halves(0, False)
            with eng.Fori(1, GROUPS) as g:
                halves(g, True)

        @block.tensor
        def _(eng):
            with eng.Fori(0, GROUPS) as g:
                blocks = tile_blocks(nc, eng, m.src_block, g * U)
                for j in range(U):
                    h, at = j // HU, j % HU * P
                    if at == 0:
                        eng.wait_ge(hot, g * 2 + (h + 1))
                    eng.wait_ge(used, g * U + (j + 1))
                    for k in range(3):
                        mm = eng.matmul(m.bank[j][:, 0:D], onehot[h][:, at:at + P], m.q[k][:, bass.ds(blocks[j] * D, D)],
                                        start=(k == 0), stop=(k == 2))
                    mm.then_inc(near, 1)

        @block.vector
        def _(eng):
            eng.sem_inc(used, U)

            def one_hots(g, h):
                eng.wait_ge(laid[h], g * 16 + 16)
                eng.tensor_scalar(onehot[h], lines_in[h], m.lane_id[0:BN, 0:1], None, ALU.is_equal).then_inc(hot, 1)

            def mix(g, j):
                eng.wait_ge(near, g * U + (j + 1))
                eng.wait_ge(gathered[j], g * 16 + 16)
                eng.tensor_tensor(m.work[:, j, :], m.bank[j][:, 0:D], m.rows[:, j, 0:D], ALU.mult).then_inc(used, 1)

            def heads(g, j):
                eng.wait_ge(used, g * U + (U + j + 1))
                eng.tensor_reduce(m.S[:, bass.ds(g * U + j, 1), :].rearrange("p a h -> p (a h)"),
                                  m.work[:, j, :].rearrange("p (h d) -> p h d", h=HEADS), AX.X, ALU.add).then_inc(mixed, 1)

            def group(g, more):
                for j in range(U):
                    mix(g, j)
                    if more and j % HU == HU - 1:
                        one_hots(g + 1, j // HU)
                    if j:
                        heads(g, j - 1)
                heads(g, U - 1)

            for h in range(2):
                one_hots(0, h)
            with eng.Fori(0, GROUPS - 1) as g:
                group(g, True)
            group(GROUPS - 1, False)


def additive_scores(nc, m, lines):
    HE, STEPS = 4 * P, TILES // 4
    CS = PU // 8
    BODY = 2 * CS
    R3 = 3 * NB
    with Phase(nc) as ctx:
        sem = ctx.sem
        laid = [sem("laid0"), sem("laid1")]
        hot, hot_too, gap = sem("hot"), sem("hot_too"), sem("gap")
        begun = sem("begun")
        looked, masked, summed, kept, step = sem("looked"), sem("masked"), sem("summed"), sem("kept"), sem("step")
        block = ctx.block()
        chunks = [t[:, 0:BODY * HE].bitcast(F16).rearrange("p (w k e) -> p w k e", w=2, k=2) for t in (m.node, m.acc)]
        lanes, blocks = chunks[0][0:BN, :, :, :], chunks[1][0:R3, :, :, :]
        onehot = [m.hots[0:BN, h, :, :] for h in range(2)]
        wide = m.work[:, :, :].rearrange("p a b -> p (a b)")
        apart = [wide[0:BN, 2 * HE + h * HE // 2:2 * HE + (h + 1) * HE // 2].bitcast(F16) for h in range(2)]
        own = [wide[0:R3, h * HE:(h + 1) * HE].bitcast(BF16).rearrange("p (k e) -> p k e", k=2) for h in range(2)]

        def of_step(numbers, k, u):
            u %= BODY
            return numbers[:, u // CS, k, u % CS * HE:(u % CS + 1) * HE]

        @block.sync
        def _(eng):
            def load(i, later):
                for w in range(2):
                    if later:
                        eng.wait_ge(masked, i * BODY + (w - 1) * CS)
                    at = bass.ds((i * 2 + w) * (CS * HE), CS * HE)
                    eng.dma_start(lanes[:, w, :, :], lines[0:2, at].partition_broadcast(BN)).then_inc(laid[w], 16)
                    eng.dma_start(blocks[:, w, :, :], lines[2:4, at].partition_broadcast(R3)).then_inc(laid[w], 16)

            load(0, False)
            with eng.Fori(1, STEPS // BODY) as i:
                load(i, True)

        @block.gpsimd
        def _(eng):
            def source_hots(i, later):
                for u in range(BODY):
                    if u % CS == 0:
                        eng.wait_ge(laid[u // CS], i * 32 + 32)
                    if later or u >= 2:
                        eng.wait_ge(looked, i * BODY + (u - 1))
                    eng.sem_inc(begun, 1)
                    eng.tensor_scalar(onehot[u % 2][:, 0, :], of_step(lanes, 0, u), m.lane_id[0:BN, 0:1], None,
                                      ALU.is_equal).then_inc(hot, 1)

            source_hots(0, False)
            with eng.Fori(1, STEPS // BODY) as i:
                source_hots(i, True)

        @block.scalar
        def _(eng):
            def target_hots(i, later):
                for u in range(BODY):
                    if u % CS == 0:
                        eng.wait_ge(laid[u // CS], i * 32 + 32)
                    eng.activation(apart[u % 2], of_step(lanes, 1, u), ACT.Abs, scale=-1.0, bias=m.lane_id[0:BN, 0:1]).then_inc(gap, 1)
                    if later or u >= 2:
                        eng.wait_ge(looked, i * BODY + (u - 1))
                    eng.wait_ge(gap, i * BODY + (u + 1))
                    eng.activation(onehot[u % 2][:, 1, :], apart[u % 2], ACT.Relu, scale=-1.0, bias=m.ones[0:BN, 0:1]).then_inc(hot_too, 1)

            eng.activation(m.small[:, 4, P - 1:P], m.zeros_b[:, 0:1], ACT.Relu)
            target_hots(0, False)
            with eng.Fori(1, STEPS // BODY) as i:
                target_hots(i, True)

        @block.tensor
        def _(eng):
            def look(n, h):
                eng.wait_ge(hot, n + 1)
                eng.wait_ge(hot_too, n + 1)
                for k in range(2):
                    mm = eng.matmul(m.bank[2 * h + k][0:R3, :], m.parts[:, k, :], onehot[h][:, k, :], start=True, stop=True)
                mm.then_inc(looked, 1)

            def add(n, h, later=True):
                eng.wait_ge(masked, n + 1)
                if later:
                    eng.wait_ge(kept, n - 1)
                for j in range(4):
                    for k in range(2):
                        mm = eng.matmul(m.bank[4 + h][:, j:j + 1], own[h][:, k, j * P:(j + 1) * P], m.behind[0:R3, 0:1],
                                        start=(k == 0), stop=(k == 1))
                mm.then_inc(summed, 1)

            look(0, 0)
            look(1, 1)
            for n in range(2):
                add(n, n, False)
                look(n + 2, n)
            with eng.Fori(1, STEPS // 2 - 1) as i:
                for h in range(2):
                    add(i * 2 + h, h)
                    look(i * 2 + (h + 2), h)
            for h in range(2):
                add(STEPS - 2 + h, h)

        @block.vector
        def _(eng):
            def mask(i, u):
                eng.wait_ge(looked, i * BODY + (u + 1))
                for k in range(2):
                    ins = eng.scalar_tensor_tensor(out=own[u % 2][:, k, :], in0=of_step(blocks, k, u), scalar=m.lane_id[0:R3, 1:2],
                                                   in1=m.bank[2 * (u % 2) + k][0:R3, :], op0=ALU.is_equal, op1=ALU.mult)
                ins.then_inc(masked, 1)

            def keep(i, u):
                eng.wait_ge(summed, i * BODY + (u + 1))
                eng.tensor_copy(m.S1[:, bass.ds((i * BODY + u) * 4, 4)], m.bank[4 + u % 2][:, 0:4]).then_inc(kept, 1)

            mask(0, 0)
            with eng.Fori(0, STEPS // BODY - 1) as i:
                for u in range(BODY):
                    mask(i, u + 1)
                    keep(i, u)
            last = STEPS // BODY - 1
            for u in range(BODY):
                if u + 1 < BODY:
                    mask(last, u + 1)
                keep(last, u)
            eng.wait_ge(kept, STEPS)
            eng.scalar_tensor_tensor(out=m.S1[:, :], in0=m.S1[:, :], scalar=0.01, in1=m.S1[:, :],
                                     op0=ALU.mult, op1=ALU.max).then_inc(step, 1)
            eng.wait_ge(step, 1)


def softmax_weights(nc, m, H, scores, maxima, scale):
    L = CH * H
    with Phase(nc) as ctx:
        sem = ctx.sem
        keys, turned, evacuated, scored, stepped = sem("keys"), sem("turned"), sem("evacuated"), sem("scored"), sem("stepped")
        step, ends, ends_turned, carried, carried_turned = sem("step"), sem("ends"), sem("ends_turned"), sem("carried"), sem("carried_turned")
        done, subtracted = sem("done"), sem("subtracted")
        block = ctx.block()
        wide_key = maxima
        steps = m.acc[0:L, 0:CU + 1]
        vals = m.node[0:L, 0:CU]
        col = m.small[0:L, 4, 0:8]
        row = m.small[0:1, 0:4, :]

        def turn_in(eng, of, j, n):
            return eng.transpose(m.bank[n % 4][0:L, 0:P], of[:, j * CH:(j + 1) * CH, :].rearrange("p c h -> p (c h)"),
                                 m.ident[:, :])

        @block.tensor
        def _(eng):
            eng.wait_ge(keys, 1)
            for j in range(CT):
                if j >= 4:
                    eng.wait_ge(evacuated, j - 3)
                turn_in(eng, wide_key, j, j).then_inc(turned, 1)
            for j in range(CT):
                eng.wait_ge(evacuated, CT + j - 3)
                turn_in(eng, scores, j, CT + j).then_inc(turned, 1)
            for way in range(2):
                eng.wait_ge(ends, way + 1)
                for k in range(4):
                    tr = eng.transpose(m.bank[4 + k][0:1, 0:L], col[:, (0, 1, 2, 3 + way)[k]:(0, 1, 2, 3 + way)[k] + 1],
                                       m.ident[0:L, 0:L])
                tr.then_inc(ends_turned, 1)
                eng.wait_ge(carried, way + 1)
                eng.transpose(m.bank[4][0:L, 0:1], row[:, 3, 0:L], m.ident[0:1, 0:1]).then_inc(carried_turned, 1)
            eng.wait_ge(scored, 1)
            for j in range(CT):
                eng.wait_ge(evacuated, 2 * CT + j - 3)
                eng.transpose(m.bank[(2 * CT + j) % 4][:, 0:L], vals[:, j * P:(j + 1) * P], m.ident[0:L, 0:L]).then_inc(turned, 1)

        @block.scalar
        def _(eng):
            for j in range(CT):
                eng.wait_ge(turned, j + 1)
                eng.activation(vals[:, j * P:(j + 1) * P], m.bank[j % 4][0:L, 0:P], ACT.Copy).then_inc(evacuated, 1)
            eng.wait_ge(stepped, 1)
            for j in range(CT):
                eng.wait_ge(turned, CT + j + 1)
                eng.activation(vals[:, j * P:(j + 1) * P], m.bank[(CT + j) % 4][0:L, 0:P], ACT.Copy).then_inc(evacuated, 1)
            for j in range(CT):
                eng.wait_ge(turned, 2 * CT + j + 1)
                eng.activation(maxima[:, j * CH:(j + 1) * CH, :], m.bank[(2 * CT + j) % 4][:, 0:L].rearrange("p (c h) -> p c h", c=CH),
                               ACT.Copy).then_inc(evacuated, 1)
            eng.wait_ge(subtracted, 1)
            eng.activation(scores, scores, ACT.Exp, scale=scale).then_inc(done, 1)

        @block.vector
        def _(eng):
            c = Count()

            def do(ins):
                ins.then_inc(step, 1)
                eng.wait_ge(step, c.up())

            eng.tensor_copy(wide_key, bcast(m.src_key[:, :], 2, H)).then_inc(keys, 1)
            do(eng.memset(steps[:, 0:1], 0.0))
            do(eng.memset(steps[:, CU:CU + 1], 0.0))
            eng.wait_ge(evacuated, CT)
            do(eng.tensor_tensor(steps[:, 1:CU], vals[:, 0:CU - 1], vals[:, 1:CU], ALU.subtract))
            do(eng.tensor_copy(col[:, 0:1], vals[:, 0:1]))
            do(eng.tensor_copy(col[:, 1:2], vals[:, CU - 1:CU]))
            do(eng.tensor_tensor(col[:, 2:3], col[:, 0:1], col[:, 1:2], ALU.subtract))
            eng.sem_inc(stepped, 1)
            eng.wait_ge(evacuated, 2 * CT)
            for way in range(2):
                if way == 0:
                    do(eng.tensor_tensor_scan(vals, steps[:, 0:CU], vals, -BIG, ALU.add, ALU.max))
                    do(eng.tensor_copy(col[:, 3:4], vals[:, CU - 1:CU]))
                else:
                    do(eng.tensor_tensor_scan(vals[:, ::-1], steps[:, CU:0:-1], vals[:, ::-1], -BIG, ALU.add, ALU.max))
                    do(eng.tensor_copy(col[:, 4:5], vals[:, 0:1]))
                eng.sem_inc(ends, 1)
                eng.wait_ge(ends_turned, way + 1)
                first, final, alone, end = [m.bank[4 + k][0:1, 0:L].rearrange("p (c h) -> p h c", c=CH) for k in range(4)]
                a = row[:, 0, 0:L].rearrange("p (h c) -> p h c", h=H)
                b = row[:, 1, 0:L].rearrange("p (h c) -> p h c", h=H)
                s = row[:, 2, 0:L].rearrange("p (h c) -> p h c", h=H)
                firsts = row[:, 3, 0:L].rearrange("p (h c) -> p h c", h=H)
                do(eng.memset(row[:, 0, 0:L], 1.0))
                do(eng.tensor_copy(firsts, first))
                do(eng.tensor_tensor(a[:, :, 1:CH], firsts[:, :, 1:CH], final[:, :, 0:CH - 1], ALU.not_equal))
                do(eng.tensor_scalar(row[:, 0, 0:L], row[:, 0, 0:L], -BIG, None, ALU.mult))
                if way == 0:
                    do(eng.tensor_copy(b, a))
                    do(eng.tensor_tensor(b[:, :, 1:CH], a[:, :, 1:CH], end[:, :, 0:CH - 1], ALU.add))
                    do(eng.tensor_tensor(a[:, :, 1:CH], a[:, :, 1:CH], alone[:, :, 0:CH - 1], ALU.add))
                    do(eng.tensor_tensor_scan(row[:, 2, 0:L], row[:, 0, 0:L], row[:, 1, 0:L], -BIG, ALU.add, ALU.max))
                else:
                    do(eng.memset(row[:, 1, 0:L], -BIG))
                    do(eng.tensor_tensor(b[:, :, 0:CH - 1], a[:, :, 1:CH], end[:, :, 1:CH], ALU.add))
                    do(eng.memset(row[:, 3, 0:L], -BIG))
                    do(eng.tensor_tensor(firsts[:, :, 0:CH - 1], a[:, :, 1:CH], alone[:, :, 1:CH], ALU.add))
                    do(eng.tensor_tensor_scan(row[:, 2, 0:L][:, ::-1], row[:, 3, 0:L][:, ::-1], row[:, 1, 0:L][:, ::-1],
                                              -BIG, ALU.add, ALU.max))
                do(eng.tensor_copy(row[:, 3, 0:L].rearrange("p (c h) -> p h c", c=CH), s))
                eng.sem_inc(carried, 1)
                eng.wait_ge(carried_turned, way + 1)
                do(eng.tensor_copy(col[:, 5 + way:6 + way], m.bank[4][0:L, 0:1]))
                if way == 0:
                    do(eng.tensor_tensor_scan(vals, steps[:, 0:CU], vals, col[:, 5:6], ALU.add, ALU.max))
                else:
                    do(eng.tensor_tensor_scan(vals[:, ::-1], steps[:, CU:0:-1], vals[:, ::-1], col[:, 6:7], ALU.add, ALU.max))
            eng.sem_inc(scored, 1)
            eng.wait_ge(evacuated, 3 * CT)
            eng.tensor_tensor(scores, scores, maxima, ALU.subtract).then_inc(subtracted, 1)
            eng.wait_ge(done, 1)


def sum_over_edges(nc, m, near_lane, weight, tile_block, index, table, width, own=None, heads=False):
    with Phase(nc) as ctx:
        sem = ctx.sem
        gathered = [sem(f"gathered{j}") for j in range(U)]
        used, copied, issued, hot, added, owned = sem("used"), sem("copied"), sem("issued"), sem("hot"), sem("added"), sem("owned")
        apart = sem("apart")
        block = ctx.block()

        def psum(j):
            return m.bank[j][0:BN, 0:width]

        @block.gpsimd
        def _(eng):
            gather_tiles(eng, nc, m, gathered, index, table, D, used, copied, issued)

        @block.scalar
        def _(eng):
            if heads:
                eng.activation(m.small[:, 4, P - 1:P], m.zeros_b[:, 0:1], ACT.Relu)
            with eng.Fori(0, GROUPS) as g:
                for j in range(U):
                    if heads or own is not None:
                        eng.wait_ge(used, g * U + (j + 1))
                        if heads:
                            eng.activation(m.turned[:, j, 0:BN], m.lane_of[:, 0:BN], ACT.Abs, scale=-1.0,
                                           bias=near_lane[:, bass.ds(g * U + j, 1)]).then_inc(apart, 1)
                            eng.activation(m.rows[:, j, D:D + HEADS], m.S[:, bass.ds(g * U + j, 1), :].rearrange("p a h -> p (a h)"),
                                           ACT.Copy)
                            eng.wait_ge(apart, g * U + (j + 1))
                            eng.activation(m.onehot[:, j, 0:BN], m.turned[:, j, 0:BN], ACT.Relu, scale=-1.0,
                                           bias=m.ones[:, 0:1]).then_inc(owned, 1)
                        else:
                            eng.activation(m.rows[:, j, D + 1:D + 2], own[:, bass.ds(g * U + j, 1)], ACT.Copy).then_inc(owned, 1)

        @block.tensor
        def _(eng):
            eng.sem_inc(used, U)
            with eng.Fori(0, GROUPS) as g:
                for j in range(U):
                    eng.wait_ge(hot, g * U + (j + 1))
                    eng.wait_ge(gathered[j], g * 16 + 16)
                    if heads or own is not None:
                        eng.wait_ge(owned, g * U + (j + 1))
                    eng.matmul(psum(j), m.onehot[:, j, 0:BN], m.rows[:, j, 0:width], start=True, stop=True).then_inc(used, 1)

        @block.vector
        def _(eng):
            def make(g, j, tile):
                if weight is None and not heads:
                    ins = eng.tensor_scalar(m.onehot[:, j, 0:BN], m.lane_of[:, 0:BN], near_lane[:, bass.ds(tile, 1)], None,
                                            ALU.is_equal)
                elif not heads:
                    ins = eng.tensor_scalar(m.onehot[:, j, 0:BN], m.lane_of[:, 0:BN], near_lane[:, bass.ds(tile, 1)],
                                            weight[:, bass.ds(tile, 1)], ALU.is_equal, ALU.mult)
                if heads:
                    eng.wait_ge(gathered[j], g * 16 + 16)
                    rows = m.rows[:, j, 0:D].rearrange("p (h d) -> p h d", h=HEADS)
                    ins = eng.tensor_tensor(rows, rows, bcast(m.S[:, bass.ds(tile, 1), :].rearrange("p a h -> p (a h)"), 2, HD), ALU.mult)
                ins.then_inc(hot, 1)

            def add(g, j, b):
                eng.wait_ge(used, g * U + (U + j + 1))
                to = m.sums[:, bass.ds(b, 1), 0:width].rearrange("p a d -> p (a d)")
                eng.wait_ge(added, g * U + (j + 1))
                eng.tensor_tensor(to, to, psum(j), ALU.add).then_inc(added, 1)

            eng.memset(m.sums[:, :, :], 0.0).then_inc(added, 1)
            if not heads:
                eng.memset(m.rows[:, :, D:D + 1], 1.0)
            for j in range(U):
                make(0, j, j)
            with eng.Fori(0, GROUPS - 1) as g:
                blocks = tile_blocks(nc, eng, tile_block, g * U)
                for j in range(U):
                    add(g, j, blocks[j])
                    make(g + 1, j, g * U + (U + j))
            blocks = tile_blocks(nc, eng, tile_block, TILES - U)
            for j in range(U):
                add(GROUPS - 1, j, blocks[j])
            eng.wait_ge(added, TILES + 1)


def node_step(nc, build):
    with Phase(nc) as ctx:
        step = ctx.sem("step")
        block = ctx.block()

        @block.vector
        def _(eng):
            c = Count()

            def do(ins):
                ins.then_inc(step, 1)
                eng.wait_ge(step, c.up())

            build(eng, do)


def batch_norm(nc, m, A, out):
    with Phase(nc) as ctx:
        sem = ctx.sem
        loaded, step, agg_ready, centred, squared, summed = sem("loaded"), sem("step"), sem("agg_ready"), sem("centred"), sem("squared"), sem("summed")
        var_ready, root_ready, done, stored = sem("var_ready"), sem("root_ready"), sem("done"), sem("stored")
        block = ctx.block()
        sums = m.sums[:, :, 0:D]
        mean = m.work[0:BN, 0, :]
        var = m.work[0:BN, 1, :]
        bias, gamma, beta = [m.bias[:, k * D:(k + 1) * D] for k in range(3)]

        turns = [slice(i * BU, (i + 1) * BU) for i in range(NB // BU)]

        @block.sync
        def _(eng):
            for to, name in ((bias, "L3_gnn_bias"), (gamma, "L3_gnn_bn_gamma"), (beta, "L3_gnn_bn_beta")):
                eng.dma_start(to, A[name].partition_broadcast(BN)).then_inc(loaded, 16)
            for i, t in enumerate(turns):
                eng.wait_ge(done, i + 1)
                eng.dma_start(out.rearrange("(b p) d -> p b d", p=BN)[:, t, :], m.x[:, t, :]).then_inc(stored, 16)
            eng.wait_ge(stored, 16 * len(turns))

        @block.tensor
        def _(eng):
            for k, (ready, of) in enumerate(((agg_ready, m.nodes), (squared, sums))):
                for i in range(len(turns)):
                    eng.wait_ge(ready, i + 1)
                    for b in range(i * BU, (i + 1) * BU):
                        mm = eng.matmul(m.bank[k][0:BN, 0:D], m.ones[0:BN, 0:BN], of[:, b, :], start=(b == 0), stop=(b == NB - 1))
                mm.then_inc(summed, 1)

        @block.scalar
        def _(eng):
            for i, t in enumerate(turns):
                eng.wait_ge(centred, i + 1)
                eng.activation(sums[:, t, :], m.nodes[:, t, :], ACT.Square).then_inc(squared, 1)
            eng.wait_ge(var_ready, 1)
            eng.activation(var, var, ACT.Sqrt).then_inc(root_ready, 1)

        @block.vector
        def _(eng):
            c = Count()

            def do(ins):
                ins.then_inc(step, 1)
                eng.wait_ge(step, c.up())

            for i, t in enumerate(turns):
                do(eng.tensor_tensor(m.nodes[:, t, :], m.nodes[:, t, :], sums[:, t, :], ALU.add))
                do(eng.tensor_tensor(m.nodes[:, t, :], m.nodes[:, t, :], bcast(m.dinv[:, t], 2, D), ALU.mult))
                if i == 0:
                    eng.wait_ge(loaded, 48)
                eng.tensor_tensor(m.nodes[:, t, :], m.nodes[:, t, :], bcast(bias, 1, BU), ALU.add).then_inc(agg_ready, 1)
            eng.wait_ge(summed, 1)
            do(eng.tensor_scalar(mean, m.bank[0][0:BN, 0:D], 1.0 / N, None, ALU.mult))
            for t in turns:
                eng.tensor_tensor(m.nodes[:, t, :], m.nodes[:, t, :], bcast(mean, 1, BU), ALU.subtract).then_inc(centred, 1)
            eng.wait_ge(summed, 2)
            eng.tensor_scalar(var, m.bank[1][0:BN, 0:D], 1.0 / N, EPS, ALU.mult, ALU.add).then_inc(var_ready, 1)
            eng.wait_ge(root_ready, 1)
            do(eng.reciprocal(var, var))
            do(eng.tensor_tensor(var, var, gamma, ALU.mult))
            for t in turns:
                do(eng.tensor_tensor(m.nodes[:, t, :], m.nodes[:, t, :], bcast(var, 1, BU), ALU.mult))
                do(eng.tensor_tensor(m.nodes[:, t, :], m.nodes[:, t, :], bcast(beta, 1, BU), ALU.add))
                eng.scalar_tensor_tensor(out=m.x[:, t, :], in0=m.nodes[:, t, :], scalar=0.0, in1=m.x[:, t, :],
                                         op0=ALU.max, op1=ALU.add).then_inc(done, 1)


def flat(ap):
    return ap.rearrange("p b d -> p (b d)")


def turn_weights(nc, m, A):
    with Phase(nc) as ctx:
        loaded, turned, copied = [ctx.sem(n) for n in ("loaded", "turned", "copied")]
        block = ctx.block()
        raw = m.work[:, 0:2, :]

        @block.sync
        def _(eng):
            eng.dma_start(raw, A["L1_gnn_W_layer"].rearrange("(o p) i -> p o i", p=P)).then_inc(loaded, 16)

        @block.tensor
        def _(eng):
            eng.wait_ge(loaded, 16)
            for o in range(2):
                for i in range(2):
                    eng.transpose(m.bank[2 * o + i][:, 0:P], raw[:, o, i * P:(i + 1) * P], m.ident[:, :]).then_inc(turned, 1)

        @block.scalar
        def _(eng):
            for o in range(2):
                for i in range(2):
                    eng.wait_ge(turned, 2 * o + i + 1)
                    eng.activation(m.weights[:, i, o * P:(o + 1) * P], m.bank[2 * o + i][:, 0:P], ACT.Copy).then_inc(copied, 1)
            eng.wait_ge(copied, 4)


def gnn_kernel(nc, A, out, upto=99, dump=None):
    def scratch(name, rows, cols):
        return nc.dram_tensor(name, (rows, cols), F32, kind="Internal").ap()

    keys, values, feats = scratch("keys", N, D), scratch("values", N, D), scratch("feats", N, D)
    lines = nc.dram_tensor("lines", (4, TILES * P), F16, kind="Internal").ap()
    typed, shared = scratch("typed", RELS * N, D), scratch("shared", N, D)
    records = scratch("records", P * (TILES + 1), 4)

    def by_k(w):
        return w.rearrange("(k p) n -> p k n", p=P)

    with ExitStack() as ctx:
        m = Memory(nc, ctx)
        load_inputs(nc, m, A)
        sort_edges(nc, m, records)
        lay_out_ends(nc, m, lines)

        def qkv(eng, j, b, g, psum):
            if g == 0:
                return eng.tensor_tensor(m.nodes[:, bass.ds(b, 1), :].rearrange("p a d -> p (a d)"), psum, m.bias[:, 0:D], ALU.add)
            return eng.tensor_tensor(m.stage[:, j, 0:2 * D], psum, m.bias[:, D:3 * D], ALU.add)

        def blocks_of(table):
            return table.rearrange("(b p) d -> p b d", p=BN)

        def store_kv(b, j):
            for k, table in enumerate((keys, values)):
                yield (blocks_of(table)[:, bass.ds(b, 1), :].rearrange("p a d -> p (a d)"), m.stage[:, j, k * D:(k + 1) * D])

        loads = []
        for k, n in enumerate("qkv"):
            loads.append((m.weights[:, :, k * D:(k + 1) * D], by_k(A["L0_gnn_W" + n])))
            loads.append((m.bias[:, k * D:(k + 1) * D], A["L0_gnn_b" + n].partition_broadcast(BN)))
        project(nc, m, [(0, D), (D, 3 * D)], qkv, loads, store=store_kv, stored=2)
        split_q(nc, m)
        edge_scores(nc, m, keys, lines)
        if upto == 1:
            return dump(m)
        softmax_weights(nc, m, HEADS, m.S, m.M, SCALE)
        if upto == 2:
            return dump(m)
        sum_over_edges(nc, m, m.src_lane, None, m.src_block, m.src_far, values, D + HEADS, heads=True)
        loads = [(m.weights[:, :, 0:D], by_k(A["L0_gnn_Wo"])), (m.bias[:, 0:D], A["L0_gnn_bo"].partition_broadcast(BN))]

        def add_to_x(eng, j, b, g, psum):
            to = m.x[:, bass.ds(b, 1), :].rearrange("p a d -> p (a d)")
            return eng.tensor_tensor(to, to, psum, ALU.add)

        project(nc, m, [(0, D)], add_to_x, loads, divide=True)
        node_step(nc, lambda eng, do: do(eng.tensor_tensor(m.x[:, :, :], m.x[:, :, :], bcast(m.bias[:, 0:D], 1, NB), ALU.add)))
        if upto == 3:
            return dump(m)

        turn_weights(nc, m, A)

        def feature(eng, j, b, g, psum):
            return eng.tensor_tensor(m.stage[:, j, 0:D], psum, m.bias[:, 0:D], ALU.add)

        def node_scores(eng, j, b):
            for k, a in enumerate((m.a1, m.a2)):
                ins = eng.scalar_tensor_tensor(out=m.stage[:, j, (k + 1) * D:(k + 2) * D], in0=m.stage[:, j, 0:D], scalar=1.0, in1=m.wa[:, k, :],
                                         op0=ALU.mult, op1=ALU.mult, accum_out=a[:, bass.ds(b, 1)])
            return ins

        loads = [(m.bias[:, 0:D], A["L1_gnn_b_layer"].partition_broadcast(BN)),
                 (m.wa[:, 0, :], A["L1_gnn_w_a1"].rearrange("a d -> (a d)").partition_broadcast(BN)),
                 (m.wa[:, 1, :], A["L1_gnn_w_a2"].rearrange("a d -> (a d)").partition_broadcast(BN)),
                 (m.ba[:, 0:1], A["L1_gnn_b_a1"].partition_broadcast(BN)),
                 (m.ba[:, 1:2], A["L1_gnn_b_a2"].partition_broadcast(BN))]
        project(nc, m, [(0, D)], feature, loads,
                store=lambda b, j: [(blocks_of(feats)[:, bass.ds(b, 1), :].rearrange("p a d -> p (a d)"), m.stage[:, j, 0:D])],
                stored=1, after=node_scores)

        def add_biases(eng, do):
            do(eng.tensor_scalar(m.a1[:, :], m.a1[:, :], m.ba[:, 0:1], None, ALU.add))
            do(eng.tensor_scalar(m.a2[:, :], m.a2[:, :], m.ba[:, 1:2], None, ALU.add))
            for k, a in enumerate((m.a1, m.a2)):
                for part in range(3):
                    piece = m.parts[:, k, part * NB:(part + 1) * NB]
                    do(eng.tensor_copy(piece, a[:, :]))
                    if part < 2:
                        do(eng.tensor_tensor(a[:, :], a[:, :], piece, ALU.subtract))

        node_step(nc, add_biases)
        additive_scores(nc, m, lines)
        softmax_weights(nc, m, 1, m.S1.unsqueeze(2), m.M1.unsqueeze(2), 1.0)
        sum_over_edges(nc, m, m.src_lane, m.S1, m.src_block, m.src_far, feats, D + 1)

        def divided(eng, do):
            do(eng.tensor_scalar(m.rstd[:, :], m.sums[:, :, D], 0.5, None, ALU.max))
            do(eng.reciprocal(m.rstd[:, :], m.rstd[:, :]))
            do(eng.tensor_tensor(m.nodes, m.sums[:, :, 0:D], bcast(m.rstd[:, :], 2, D), ALU.mult))
            do(eng.tensor_tensor(flat(m.x[:, :, :]), flat(m.x[:, :, :]), flat(m.nodes), ALU.add))

        node_step(nc, divided)
        if upto == 4:
            return dump(m)

        def relations(eng, j, b, g, psum):
            if g == 0:
                return eng.tensor_tensor(m.nodes[:, bass.ds(b, 1), :].rearrange("p a d -> p (a d)"), psum, m.bias[:, 0:D], ALU.add)
            return eng.tensor_copy(m.stage[:, j, (g - 1) * 2 * D:g * 2 * D], psum)

        loads = [(m.weights[:, :, 0:D], by_k(A["L2_gnn_self_W"])), (m.bias[:, 0:D], A["L2_gnn_self_b"].partition_broadcast(BN))]
        for r in range(RELS):
            loads.append((m.weights[:, :, (r + 1) * D:(r + 2) * D], by_k(A["L2_gnn_rel_W"][r, :, :])))
        by_relation = typed.rearrange("(r b p) d -> p r b d", r=RELS, p=BN)
        project(nc, m, [(0, D), (D, 3 * D), (3 * D, 5 * D)], relations, loads,
                store=lambda b, j: [(by_relation[:, :, bass.ds(b, 1), :].rearrange("p r a d -> p r (a d)"),
                                     m.stage[:, j, 0:RELS * D].rearrange("p (r d) -> p r d", r=RELS))],
                stored=1)
        sum_over_edges(nc, m, m.dst_lane, None, m.dst_block, m.dst_far[:, 0, :], typed, D + 2, own=m.dst_w)

        def mean_of_edges(eng, do):
            do(eng.tensor_scalar(m.rstd[:, :], m.sums[:, :, D], 1.0, None, ALU.max))
            do(eng.reciprocal(m.rstd[:, :], m.rstd[:, :]))
            do(eng.tensor_tensor(m.sums[:, :, 0:D], m.sums[:, :, 0:D], bcast(m.rstd[:, :], 2, D), ALU.mult))
            do(eng.tensor_tensor(m.nodes, m.nodes, m.sums[:, :, 0:D], ALU.add))
            do(eng.scalar_tensor_tensor(out=flat(m.x[:, :, :]), in0=flat(m.nodes), scalar=0.0, in1=flat(m.x[:, :, :]),
                                        op0=ALU.max, op1=ALU.add))
            do(eng.tensor_scalar(m.a1[:, :], m.sums[:, :, D + 1], 1.0, None, ALU.add))
            do(eng.tensor_scalar(m.a2[:, :], m.a1[:, :], 0.0, None, ALU.is_gt))
            do(eng.tensor_scalar(m.a1[:, :], m.a1[:, :], 1e-30, None, ALU.max))

        node_step(nc, mean_of_edges)
        with Phase(nc) as inner:
            rooted = inner.sem("rooted")
            block = inner.block()

            @block.scalar
            def _(eng):
                eng.activation(m.dinv[:, :], m.a1[:, :], ACT.Sqrt).then_inc(rooted, 1)
                eng.wait_ge(rooted, 1)

        def inverse_root(eng, do):
            do(eng.reciprocal(m.dinv[:, :], m.dinv[:, :]))
            do(eng.tensor_tensor(m.dinv[:, :], m.dinv[:, :], m.a2[:, :], ALU.mult))

        node_step(nc, inverse_root)
        if upto == 5:
            return dump(m)

        def scaled(eng, j, b, g, psum):
            return eng.tensor_scalar(m.nodes[:, bass.ds(b, 1), :].rearrange("p a d -> p (a d)"), psum,
                                     m.dinv[:, bass.ds(b, 1)], None, ALU.mult)

        project(nc, m, [(0, D)], scaled, [(m.weights[:, :, 0:D], by_k(A["L3_gnn_weight"]))],
                store=lambda b, j: [(blocks_of(shared)[:, bass.ds(b, 1), :], m.nodes[:, bass.ds(b, 1), :])], stored=1)
        sum_over_edges(nc, m, m.dst_lane, m.dst_w, m.dst_block, m.dst_far[:, 1, :], shared, D)
        batch_norm(nc, m, A, out)


_INS = ["x", "src", "dst", "edge_type_4", "edge_weight", "L0_gnn_Wq", "L0_gnn_bq", "L0_gnn_Wk", "L0_gnn_bk", "L0_gnn_Wv",
        "L0_gnn_bv", "L0_gnn_Wo", "L0_gnn_bo", "L1_gnn_W_layer", "L1_gnn_b_layer", "L1_gnn_w_a1", "L1_gnn_b_a1",
        "L1_gnn_w_a2", "L1_gnn_b_a2", "L2_gnn_self_W", "L2_gnn_self_b", "L2_gnn_rel_W", "L3_gnn_weight", "L3_gnn_bias",
        "L3_gnn_bn_gamma", "L3_gnn_bn_beta"]


def kernel(**inputs):
    import numpy as np
    import concourse.bacc as bacc
    from concourse.bass_utils import run_bass_kernel_spmd

    nc = bacc.Bacc("TRN2", target_bir_lowering=False, num_devices=1)
    arrays, A = {}, {}
    for name in _INS:
        a = np.ascontiguousarray(inputs[name])
        arrays["in_" + name] = a
        A[name] = nc.dram_tensor("in_" + name, a.shape, mybir.dt.from_np(a.dtype), kind="ExternalInput").ap()
    out = nc.dram_tensor("out", (N, D), F32, kind="ExternalOutput").ap()
    gnn_kernel(nc, A, out)
    return run_bass_kernel_spmd(nc, [arrays], core_ids=[0]).results[0]["out"]
```
